# Optimizing a Trainium2 kernel written in Bass

```python
import numpy as np
import jax
import jax.numpy as jnp

def _softmax(x, axis=-1):
    return jax.nn.softmax(x, axis=axis)

def _gelu(x):
    return jax.nn.gelu(x, approximate=True)

def _silu(x):
    return jax.nn.silu(x)

def _sigmoid(x):
    return jax.nn.sigmoid(x)

def _layernorm(x, axis=-1, eps=1e-05):
    m = jnp.mean(x, axis=axis, keepdims=True)
    v = jnp.var(x, axis=axis, keepdims=True)
    return (x - m) / jnp.sqrt(v + eps)

def _scatter_add(tgt, idx, src, axis=0):
    return tgt.at[idx].add(src)

def _segment_sum(src, seg, n):
    return jax.ops.segment_sum(src, seg, n)
kernel_name = 'mk_adj_resnorm_d4_adj_r2_b24502'

def setup_inputs(seed: int=0):
    np.random.seed(seed)
    _w = jnp.asarray

    def _rec_inputs():
        import jax
        import jax.numpy as jnp
        _gk = jax.random.key(seed)
        x = -0.0002928 + 1 * jax.random.normal(jax.random.fold_in(_gk, 1), (64, 128, 256), jnp.float32)
        _a = jax.random.bernoulli(jax.random.fold_in(_gk, 2), 0.0625, (64, 128, 128))
        _a = jnp.logical_or(_a, jnp.swapaxes(_a, -1, -2))
        _a = jnp.logical_or(_a, jnp.eye(128, dtype=bool))
        adj = _a.astype(jnp.int32)
        return (x, adj)
    x, adj = _rec_inputs()

    def _L0_gnn_setup():
        import jax, jax.numpy as jnp
        import numpy as np
        L = 3
        D = 256
        B, N = (8, 512)
        EPS = 1e-05

        def layernorm(x, gamma, beta):
            mu = jnp.mean(x, axis=-1, keepdims=True)
            var = jnp.var(x, axis=-1, keepdims=True)
            return (x - mu) * jax.lax.rsqrt(var + EPS) * gamma + beta
        key = jax.random.key(seed)
        ks = jax.random.split(key, 12)
        s = 1.0 / np.sqrt(D)
        node_features = jax.random.normal(ks[0], (B, N, D), dtype=jnp.float32)
        adjacency_matrix = jax.random.randint(ks[1], (B, N, N), 0, 2, dtype=jnp.int32)
        return {'node_features': node_features, 'adjacency_matrix': adjacency_matrix, 'attn_w': jax.random.normal(ks[2], (L, 2 * D), dtype=jnp.float32) * (1.0 / np.sqrt(2 * D)), 'attn_b': jax.random.normal(ks[3], (L,), dtype=jnp.float32) * 0.01, 'W1': jax.random.normal(ks[4], (L, D, 4 * D), dtype=jnp.float32) * s, 'b1': jnp.zeros((L, 4 * D), dtype=jnp.float32), 'W2': jax.random.normal(ks[5], (L, 4 * D, D), dtype=jnp.float32) * (1.0 / np.sqrt(4 * D)), 'b2': jnp.zeros((L, D), dtype=jnp.float32), 'g1': jnp.ones((L, D), dtype=jnp.float32), 'beta1': jnp.zeros((L, D), dtype=jnp.float32), 'g2': jnp.ones((L, D), dtype=jnp.float32), 'beta2': jnp.zeros((L, D), dtype=jnp.float32)}
    _L0_gnn_all = _L0_gnn_setup()
    _L0_gnn_in = {k: v for k, v in _L0_gnn_all.items() if k in ('attn_w', 'attn_b', 'W1', 'b1', 'W2', 'b2', 'g1', 'beta1', 'g2', 'beta2')}
    del _L0_gnn_all

    def _L1_gnn_setup():
        import jax, jax.numpy as jnp
        import numpy as np
        ALPHA = 0.2
        K_NUM = 16
        NEG_INF = -9000000000000000.0
        key = jax.random.key(seed)
        k1, k2, k3, k4 = jax.random.split(key, 4)
        B, N, F_in, F_out = (4, 1024, 256, 256)
        h = jax.random.normal(k1, (B, N, F_in), dtype=jnp.float32)
        adj = jax.random.randint(k2, (B, N, N), 0, 2, dtype=jnp.int32)

        def xavier(k, shape, gain=1.414):
            fan_in, fan_out = (shape[0], shape[1])
            bound = gain * np.sqrt(6.0 / (fan_in + fan_out))
            return jax.random.uniform(k, shape, jnp.float32, -bound, bound)
        W = xavier(k3, (F_in, F_out))
        a = xavier(k4, (2 * F_out, 1))
        return {'h': h, 'adj': adj, 'W': W, 'a': a}
    _L1_gnn_all = _L1_gnn_setup()
    _L1_gnn_in = {k: v for k, v in _L1_gnn_all.items() if k in ('W', 'a')}
    del _L1_gnn_all

    def _L2_gnn_setup():
        import jax, jax.numpy as jnp
        import numpy as np
        B, N, D = (32, 128, 256)
        DIR = 2
        NUM_LABELS = 16
        key = jax.random.key(seed)
        k1, k2, k3, k4 = jax.random.split(key, 4)
        feature = jax.random.normal(k1, (B, N, D), dtype=jnp.float32)
        graph = jax.random.randint(k2, (B, N, N), 0, NUM_LABELS, dtype=jnp.int64)
        weights = jax.random.normal(k3, (DIR, D, D), dtype=jnp.float32) * (1.0 / np.sqrt(D))
        stdv = 1.0 / np.sqrt(D)
        bias = jax.random.uniform(k4, (NUM_LABELS, D), dtype=jnp.float32, minval=-stdv, maxval=stdv)
        return {'feature': feature, 'graph': graph, 'weights': weights, 'bias': bias}
    _L2_gnn_all = _L2_gnn_setup()
    _L2_gnn_in = {k: v for k, v in _L2_gnn_all.items() if k in ('weights', 'bias')}
    del _L2_gnn_all

    def _L3_gnn_setup():
        import jax, jax.numpy as jnp
        import numpy as np
        B, N, DIN, DOUT = (8, 1024, 256, 256)
        key = jax.random.key(seed)
        kx, ka, kw, kb, kattn = jax.random.split(key, 5)
        x = jax.random.normal(kx, (B, N, DIN), dtype=jnp.float32)
        adjacency_matrix = jax.random.randint(ka, (B, N, N), 0, 2, dtype=jnp.int32)
        lim_w = float(np.sqrt(1.0 / DIN))
        W = jax.random.uniform(kw, (DOUT, DIN), minval=-lim_w, maxval=lim_w, dtype=jnp.float32)
        b = jax.random.uniform(kb, (DOUT,), minval=-lim_w, maxval=lim_w, dtype=jnp.float32)
        lim_a = float(np.sqrt(6.0 / (DOUT + DOUT)))
        attn = jax.random.uniform(kattn, (DOUT, DOUT), minval=-lim_a, maxval=lim_a, dtype=jnp.float32)
        return {'x': x, 'adjacency_matrix': adjacency_matrix, 'W': W, 'b': b, 'attn': attn}
    _L3_gnn_all = _L3_gnn_setup()
    _L3_gnn_in = {k: v for k, v in _L3_gnn_all.items() if k in ('W', 'b', 'attn')}
    del _L3_gnn_all
    return {'x': x, 'adj': adj, 'L0_gnn_attn_w': _L0_gnn_in['attn_w'], 'L0_gnn_attn_b': _L0_gnn_in['attn_b'], 'L0_gnn_W1': _L0_gnn_in['W1'], 'L0_gnn_b1': _L0_gnn_in['b1'], 'L0_gnn_W2': _L0_gnn_in['W2'], 'L0_gnn_b2': _L0_gnn_in['b2'], 'L0_gnn_g1': _L0_gnn_in['g1'], 'L0_gnn_beta1': _L0_gnn_in['beta1'], 'L0_gnn_g2': _L0_gnn_in['g2'], 'L0_gnn_beta2': _L0_gnn_in['beta2'], 'L1_gnn_W': _L1_gnn_in['W'], 'L1_gnn_a': _L1_gnn_in['a'], 'L2_gnn_weights': _L2_gnn_in['weights'], 'L2_gnn_bias': _L2_gnn_in['bias'], 'L3_gnn_W': _L3_gnn_in['W'], 'L3_gnn_b': _L3_gnn_in['b'], 'L3_gnn_attn': _L3_gnn_in['attn']}

def reference(x, adj, L0_gnn_attn_w, L0_gnn_attn_b, L0_gnn_W1, L0_gnn_b1, L0_gnn_W2, L0_gnn_b2, L0_gnn_g1, L0_gnn_beta1, L0_gnn_g2, L0_gnn_beta2, L1_gnn_W, L1_gnn_a, L2_gnn_weights, L2_gnn_bias, L3_gnn_W, L3_gnn_b, L3_gnn_attn):
    import jax
    import jax.numpy as jnp

    def _L0_gnn_ref(node_features, adjacency_matrix, attn_w, attn_b, W1, b1, W2, b2, g1, beta1, g2, beta2):
        import jax, jax.numpy as jnp
        import numpy as np
        L = 3
        D = 256
        B, N = (8, 512)
        EPS = 1e-05

        def layernorm(x, gamma, beta):
            mu = jnp.mean(x, axis=-1, keepdims=True)
            var = jnp.var(x, axis=-1, keepdims=True)
            return (x - mu) * jax.lax.rsqrt(var + EPS) * gamma + beta
        n = adjacency_matrix.shape[-1]
        mask = adjacency_matrix.astype(jnp.float32) + jnp.eye(n, dtype=jnp.float32) > 0
        x = node_features
        d = x.shape[-1]
        for l in range(attn_w.shape[0]):
            si = x @ attn_w[l, :d]
            sj = x @ attn_w[l, d:]
            scores = si[:, :, None] + sj[:, None, :] + attn_b[l]
            scores = jnp.where(scores >= 0, scores, 0.2 * scores)
            scores = jnp.where(mask, scores, -jnp.inf)
            attn = jax.nn.softmax(scores, axis=-1)
            agg = jnp.einsum('bij,bjd->bid', attn, x)
            h = layernorm(x + agg, g1[l], beta1[l])
            ff = jax.nn.gelu(h @ W1[l] + b1[l], approximate=False) @ W2[l] + b2[l]
            x = layernorm(h + ff, g2[l], beta2[l])
        return x

    def _L1_gnn_ref(h, adj, W, a):
        import jax, jax.numpy as jnp
        import numpy as np
        ALPHA = 0.2
        K_NUM = 16
        NEG_INF = -9000000000000000.0
        F_out = W.shape[1]
        Wh = jnp.einsum('bnf,fo->bno', h, W)
        a1, a2 = (a[:F_out, 0], a[F_out:, 0])
        e_src = Wh @ a1
        e_dst = Wh @ a2
        e = e_src[:, :, None] + e_dst[:, None, :]
        e = jnp.where(e > 0, e, ALPHA * e)
        e = jnp.where(adj > 0, e, NEG_INF)
        attention = jax.nn.softmax(e, axis=2)
        topk_vals = jax.lax.top_k(attention, K_NUM)[0]
        kth = topk_vals[:, :, -1:]
        attention = jnp.where(attention < kth, 0.0, attention)
        h_prime = jnp.einsum('bij,bjo->bio', attention, Wh)
        return jax.nn.elu(h_prime)

    def _L2_gnn_ref(feature, graph, weights, bias):
        import jax, jax.numpy as jnp
        import numpy as np
        B, N, D = (32, 128, 256)
        DIR = 2
        NUM_LABELS = 16
        out = feature + jnp.einsum('bni,doi->bno', feature, weights)
        out = out + jnp.take(bias, graph, axis=0).sum(axis=2)
        return out

    def _L3_gnn_ref(x, adjacency_matrix, W, b, attn):
        import jax, jax.numpy as jnp
        import numpy as np
        B, N, DIN, DOUT = (8, 1024, 256, 256)
        h = jnp.einsum('bni,oi->bno', x, W) + b
        ha = jnp.einsum('bmi,ij->bmj', h, attn)
        scores = jnp.einsum('bmj,bnj->bmn', ha, h)
        scores = jnp.where(adjacency_matrix == 0, -jnp.inf, scores)
        attn_weights = jax.nn.softmax(scores, axis=-1)
        x_out = jnp.einsum('bmn,bnd->bmd', attn_weights, h)
        return jax.nn.elu(x_out)
    x = _layernorm(x + _L0_gnn_ref(x, adj, L0_gnn_attn_w, L0_gnn_attn_b, L0_gnn_W1, L0_gnn_b1, L0_gnn_W2, L0_gnn_b2, L0_gnn_g1, L0_gnn_beta1, L0_gnn_g2, L0_gnn_beta2), axis=-1)
    x = _layernorm(x + _L1_gnn_ref(x, adj, L1_gnn_W, L1_gnn_a), axis=-1)
    x = _layernorm(x + _L2_gnn_ref(x, adj, L2_gnn_weights, L2_gnn_bias), axis=-1)
    x = _layernorm(x + _L3_gnn_ref(x, adj, L3_gnn_W, L3_gnn_b, L3_gnn_attn), axis=-1)
    return x

_drawn_inputs = setup_inputs


def setup_inputs(seed=0):
    import zlib

    import numpy as np

    out = dict(_drawn_inputs(seed))
    spreads = {'L0_gnn_b1': (0.0, 0.1),
     'L0_gnn_b2': (0.0, 0.1),
     'L0_gnn_g1': (1.0, 0.2),
     'L0_gnn_beta1': (0.0, 0.1),
     'L0_gnn_g2': (1.0, 0.2),
     'L0_gnn_beta2': (0.0, 0.1)}
    factors = {'L0_gnn_attn_b': 196.755}
    for name, (base, spread) in spreads.items():
        noise = np.random.default_rng([zlib.crc32(name.encode()), seed]).standard_normal(out[name].shape)
        drawn = base * np.exp(spread * noise) if base else spread * noise
        out[name] = jnp.asarray(drawn.astype(out[name].dtype))
    for name, factor in factors.items():
        out[name] = (out[name] * factor).astype(out[name].dtype)
    return out
```

```python
import concourse.bass as bass
from concourse import mybir
from contextlib import ExitStack

F32, F16, BF16, I32 = mybir.dt.float32, mybir.dt.float16, mybir.dt.bfloat16, mybir.dt.int32
ALU, ACT, AX = mybir.AluOpType, mybir.ActivationFunctionType, mybir.AxisListType

B, N, D = 64, 128, 256
G = 4
NG = B // G
T = G * N
L = 3
KD = D // 128
H = 4 * D
KH = H // 128
STEPS = L * NG
EPS = 1e-5
SLOPE = 0.2
FAR = 9e15
WS = 64.0
HB = 3


def first_network(nc, xs, ident, half, bank, x, adj, attn_w, attn_b, w1, b1_down, w2, b2, g1, beta1, g2, beta2, g1_down, beta1_down):
    ctx = ExitStack()
    with ctx:
        def sb(name, shape, dt=F32):
            return ctx.enter_context(nc.sbuf_tensor(name, shape, dt))

        def sem(name):
            return ctx.enter_context(nc.semaphore(name))

        mask = sb("mask", [128, NG, G, N], BF16)
        w1h = sb("w1h", [128, L, KD, H], F16)
        w1l = sb("w1l", [128, L, KD, H], F16)
        w2h = sb("w2h", [128, L, KH, D], F16)
        w2l = sb("w2l", [128, L, KH, D], F16)
        aw = sb("aw", [128, L, 2 * D])
        ab = sb("ab", [128, L])
        g1b = sb("g1b", [128, L, D])
        betab = sb("betab", [128, L, D])
        g2b = sb("g2b", [128, L, D])
        beta2b = sb("beta2b", [128, L, D])
        b1c = sb("b1c", [128, L, KH])
        g1c = sb("g1c", [128, L, KD])
        beta1c = sb("beta1c", [128, L, KD])
        gt = sb("gt", [128, 2, KH, T], F16)
        stage = gt[:, :, :, :].rearrange("p a k t -> p (a k t)").bitcast(F32)
        ht = sb("ht", [128, 2, KD, T], F16)
        htf = sb("htf", [128, KD, T])
        g32 = sb("g32", [128, HB, T])
        z = sb("z", [128, G, D])
        z2 = sb("z2", [128, G, D])
        hb = sb("hb", [128, 2, G, D])
        v = sb("v", [128, G, N])
        pts = sb("pts", [128, G, N])
        junk = sb("junk", [128, 2, D])
        junk_b2 = hb[:, 0, 0:3, :]
        adji = z[:, :, :].rearrange("p g d -> p (g d)").rearrange("p (b g n) -> p b g n", b=2, g=G).bitcast(I32)
        edge = z2[:, 0:2, :].rearrange("p a (b n) -> p (a b) n", b=2)
        sij = sb("sij", [128, 2 * G])
        nm = sb("nm", [128, G])
        rs = sb("rs", [128, G])
        rinv = sb("rinv", [128, G])
        st1 = sb("st1", [128, G, 6])
        mv1 = sb("mv1", [128, G, 2])
        ve1 = sb("ve1", [128, G])
        rstd1 = sb("rstd1", [128, G])
        st2 = sb("st2", [128, G, 6])
        mv2 = sb("mv2", [128, G, 2])
        ve2 = sb("ve2", [128, G])
        rstd2 = sb("rstd2", [128, G])

        hid = bank[0:HB]
        ff = bank[3:5]
        agg = bank[5:7]
        sp = bank[7]

        def pair(banks, g):
            return banks[g // 2][:, (g % 2) * D:(g % 2 + 1) * D]

        par_in = sem("par_in")
        w_in = [sem(f"w_in{i}") for i in range(2)]
        x_in = [sem(f"x_in{i}") for i in range(2)]
        adj_in = [sem(f"adj_in{i}") for i in range(2)]
        adj_used = sem("adj_used")
        w_used = sem("w_used")
        w_split = sem("w_split")
        const_ready = sem("const_ready")
        init_chain = sem("init_chain")
        x_ready = sem("x_ready")
        cols_done = sem("cols_done")
        spread_ready = sem("spread_ready")
        scores_ready = sem("scores_ready")
        score_chain = sem("score_chain")
        exp_done = sem("exp_done")
        rinv_ready = sem("rinv_ready")
        pt_ready = sem("pt_ready")
        pt_copied = sem("pt_copied")
        agg_ready = sem("agg_ready")
        ln1_chain = sem("ln1_chain")
        var1_ready = sem("var1_ready")
        rstd1_ready = sem("rstd1_ready")
        z_ready = sem("z_ready")
        ht_ready = sem("ht_ready")
        hth_done = sem("hth_done")
        htl_done = sem("htl_done")
        hb_chain = sem("hb_chain")
        hb_ready = sem("hb_ready")
        hid_ready = sem("hid_ready")
        gelu_done = sem("gelu_done")
        gh_done = sem("gh_done")
        gl_done = sem("gl_done")
        ff_ready = sem("ff_ready")
        ln2_chain = sem("ln2_chain")
        var2_ready = sem("var2_ready")
        rstd2_ready = sem("rstd2_ready")
        z2_ready = sem("z2_ready")
        x_chain = sem("x_chain")
        x_stored = sem("x_stored")

        block = ctx.enter_context(nc.Block())

        @block.sync
        def _(eng):
            def load_w(l):
                eng.dma_start(stage[:, 0:2048].rearrange("p (k h) -> p k h", k=KD),
                              w1[l].rearrange("(k p) h -> p k h", p=128)).then_inc(w_in[0], 16)
                eng.dma_start(stage[:, 2048:4096].rearrange("p (k d) -> p k d", k=KH),
                              w2[l].rearrange("(k p) d -> p k d", p=128)).then_inc(w_in[1], 16)

            def load_adj(g, b):
                eng.dma_start(adji[:, b, :, :], adj[g].rearrange("g i j -> i g j")).then_inc(adj_in[b], 16)

            def load_x(g, b):
                eng.dma_start(xs[:, g, :, :], x[g].rearrange("g n d -> n g d")).then_inc(x_in[b], 16)

            load_w(0)
            load_adj(0, 0)
            load_adj(1, 1)
            load_x(0, 0)
            load_x(1, 1)
            for g in range(2, NG):
                eng.wait_ge(adj_used, g - 1)
                load_adj(g, g % 2)
            for l in range(1, L):
                eng.wait_ge(w_used, 2 * l)
                eng.wait_ge(w_split, 2 * l)
                load_w(l)
            for g in range(NG):
                eng.wait_ge(x_in[g % 2], 16 * (g // 2 + 1))
                eng.sem_inc(x_ready, 1)
                if g + 2 < NG:
                    load_x(g + 2, g % 2)
            with eng.Fori(NG, STEPS) as s:
                eng.wait_ge(x_stored, s - (NG - 1))
                eng.sem_inc(x_ready, 1)

        @block.gpsimd
        def _(eng):
            eng.memset(ident[:, :], 0.0).then_inc(init_chain, 1)
            eng.memset(half[:, :], -0.5).then_inc(const_ready, 1)
            eng.wait_ge(init_chain, 1)
            eng.affine_select(out=ident[:, :], in_=ident[:, :], compare_op=ALU.not_equal, fill=1.0,
                              base=0, pattern=[[-1, 128]], channel_multiplier=1).then_inc(const_ready, 1)
            for tile, src in ((aw, attn_w), (g1b, g1), (betab, beta1), (junk_b2, b2), (g2b, g2), (beta2b, beta2)):
                eng.dma_start(tile[:, :, :], src.partition_broadcast(128)).then_inc(par_in, 16)
            eng.dma_start(ab[:, :], attn_b.partition_broadcast(128)).then_inc(par_in, 16)
            for tile, src in ((b1c, b1_down), (g1c, g1_down), (beta1c, beta1_down)):
                eng.dma_start(tile[:, :, :], src).then_inc(par_in, 16)
            eng.wait_ge(par_in, 16 * 10)
            eng.tensor_tensor(out=betab[:, :, :], in0=betab[:, :, :], in1=junk_b2[:, :, :], op=ALU.add)\
               .then_inc(hb_chain, 1)

            def wide(t, l):
                return t[:, l, :].unsqueeze(1).to_broadcast([128, G, D])

            def root(var_ready, rstd_ready, ve, rstd, s):
                eng.wait_ge(var_ready, s + 1)
                eng.tensor_tensor(out=rstd[:, :], in0=ve[:, :], in1=half[:, :], op=ALU.pow).then_inc(rstd_ready, 1)

            def gain1(s, l):
                eng.wait_ge(z_ready, s + 1)
                eng.tensor_tensor(out=hb[:, s & 1, :, :], in0=z[:, :, :], in1=wide(g1b, l), op=ALU.mult)\
                   .then_inc(hb_chain, 1)
                eng.wait_ge(hb_chain, s + 2)
                eng.tensor_tensor(out=hb[:, s & 1, :, :], in0=hb[:, s & 1, :, :], in1=wide(betab, l), op=ALU.add)\
                   .then_inc(hb_ready, 1)

            def gain2(s, slot, l):
                eng.wait_ge(z2_ready, s + 1)
                eng.tensor_tensor(out=xs[:, slot, :, :], in0=z2[:, :, :], in1=wide(g2b, l), op=ALU.mult)\
                   .then_inc(x_chain, 1)
                eng.wait_ge(x_chain, s + 1)
                eng.tensor_tensor(out=xs[:, slot, :, :], in0=xs[:, slot, :, :], in1=wide(beta2b, l), op=ALU.add)\
                   .then_inc(x_stored, 1)

            root(var1_ready, rstd1_ready, ve1, rstd1, 0)
            gain1(0, 0)

            def step(t, first=False, last=False):
                if not first:
                    u = t - 1
                    root(var2_ready, rstd2_ready, ve2, rstd2, u)
                    gain2(u, u & (NG - 1), layer(u))
                if not last:
                    s = t + 1
                    root(var1_ready, rstd1_ready, ve1, rstd1, s)
                    gain1(s, layer(s))

            step(0, first=True)
            with eng.Fori(1, STEPS - 1) as t:
                step(t)
            step(STEPS - 1, last=True)
            root(var2_ready, rstd2_ready, ve2, rstd2, STEPS - 1)
            gain2(STEPS - 1, NG - 1, L - 1)

        @block.scalar
        def _(eng):
            for l in range(L):
                for i, dst in enumerate((w1h, w2h)):
                    eng.wait_ge(w_in[i], 16 * (l + 1))
                    eng.activation(dst[:, l, :, :].rearrange("p k h -> p (k h)"), stage[:, 2048 * i:2048 * (i + 1)],
                                   ACT.Copy, scale=WS).then_inc(w_used, 1)

            def exps(s):
                eng.wait_ge(scores_ready, s + 1)
                for g in range(G):
                    ins = eng.activation(v[:, g, :], v[:, g, :], ACT.Exp, bias=nm[:, g:g + 1],
                                         accum_out=rs[:, g:g + 1])
                ins.then_inc(exp_done, 1)

            def heads(s, l):
                for k in range(KD):
                    eng.wait_ge(ht_ready, KD * s + k + 1)
                    sc, bi = g1c[:, l, k:k + 1], beta1c[:, l, k:k + 1]
                    eng.activation(ht[:, 0, k, :], agg[k][:, :], ACT.Identity, scale=sc, bias=bi)
                    eng.activation(htf[:, k, :], agg[k][:, :], ACT.Identity, scale=sc, bias=bi).then_inc(hth_done, 1)

            def gelus(t, l, first=False):
                if not first:
                    eng.wait_ge(ff_ready, G * t)
                for m in range(KH):
                    eng.wait_ge(hid_ready, KH * t + m + 1)
                    if not (first and m < HB):
                        eng.wait_ge(gl_done, KH * t + reuse(m))
                    eng.activation(g32[:, m % HB, :], hid[m % HB][:, :], ACT.Gelu, scale=1.0 / WS,
                                   bias=b1c[:, l, m:m + 1]).then_inc(gelu_done, 1)
                    eng.wait_ge(gelu_done, KH * t + m + 1)
                    eng.activation(gt[:, 0, m, :], g32[:, m % HB, :], ACT.Copy).then_inc(gh_done, 1)

            eng.wait_ge(par_in, 16 * 10)
            exps(0)
            heads(0, 0)
            exps(1)
            gelus(0, 0, first=True)
            exps(2)
            heads(1, 0)
            with eng.Fori(1, STEPS - 2) as t:
                gelus(t, layer(t))
                exps(t + 2)
                heads(t + 1, layer(t + 1))
            gelus(STEPS - 2, L - 1)
            heads(STEPS - 1, L - 1)
            gelus(STEPS - 1, L - 1)

        @block.tensor
        def _(eng):
            def spread(s):
                eng.wait_ge(cols_done, 2 * G * (s + 1))
                for g in range(G):
                    ins = eng.matmul(sp[:, g * N:(g + 1) * N], sij[:, G + g:G + g + 1].to_broadcast([128, 128]),
                                     ident[:, :], start=True, stop=True)
                ins.then_inc(spread_ready, 1)

            def turn(s):
                eng.wait_ge(exp_done, s + 1)
                for g in range(G):
                    ins = eng.transpose(sp[:, g * N:(g + 1) * N], v[:, g, :], ident[:, :])
                ins.then_inc(pt_ready, 1)

            def gather(s, slot, first=False):
                eng.wait_ge(pt_copied, s + 1)
                eng.wait_ge(x_ready, s + 1)
                if not first:
                    eng.wait_ge(hth_done, KD * s)
                for g in range(G):
                    eng.matmul(pair(agg, g), pts[:, g, :], xs[:, slot, g, :], start=True, stop=True)\
                       .then_inc(agg_ready, 1)

            def heads(s):
                eng.wait_ge(z_ready, s + 1)
                for k in range(KD):
                    for g in range(G):
                        ins = eng.transpose(agg[k][:, g * N:(g + 1) * N], z[:, g, k * 128:(k + 1) * 128], ident[:, :])
                    ins.then_inc(ht_ready, 1)

            def up(t, l, first=False):
                for m in range(KH):
                    if m == 0:
                        eng.wait_ge(hth_done, KD * (t + 1))
                        eng.wait_ge(htl_done, KD * (t + 1))
                    if not (first and m < HB):
                        eng.wait_ge(gelu_done, KH * t + reuse(m))
                    n = 0
                    for k in range(KD):
                        for w, a in ((w1h, 0), (w1h, 1), (w1l, 0)):
                            ins = eng.matmul(hid[m % HB][:, :], w[:, l, k, m * 128:(m + 1) * 128], ht[:, a, k, :],
                                             start=(n == 0), stop=(n == 3 * KD - 1))
                            n += 1
                    ins.then_inc(hid_ready, 1)

            def down(t, l, g, first=False):
                if g == 0 and not first:
                    eng.wait_ge(z2_ready, t)
                for k in range(KH):
                    eng.wait_ge(gh_done, KH * t + k + 1) if g == 0 else None
                    eng.wait_ge(gl_done, KH * t + k + 1) if g == 0 else None
                    for a, w in ((0, w2h), (0, w2l), (1, w2h)):
                        ins = eng.matmul(pair(ff, g), gt[:, a, k, g * N:(g + 1) * N], w[:, l, k, :],
                                         start=(k == 0 and a == 0 and w is w2h), stop=(k == KH - 1 and a == 1))
                ins.then_inc(ff_ready, 1)

            eng.wait_ge(const_ready, 2)
            spread(0)
            turn(0)
            gather(0, 0, first=True)
            heads(0)
            spread(1)

            def step(t, l, first=False, more=2):
                up(t, l, first)
                if more >= 1:
                    turn(t + 1)
                    gather(t + 1, (t + 1) & (NG - 1))
                if more >= 2:
                    spread(t + 2)
                for g in range(G):
                    down(t, l, g, first)
                    if g == G - 2 and more >= 1:
                        heads(t + 1)

            eng.wait_ge(w_used, 2 * L)
            eng.wait_ge(w_split, 2 * L)
            step(0, 0, first=True)
            with eng.Fori(1, STEPS - 2) as t:
                step(t, layer(t))
            step(STEPS - 2, L - 1, more=1)
            step(STEPS - 1, L - 1, more=0)

        @block.vector
        def _(eng):
            def low_half(l, i, dst, high):
                eng.wait_ge(w_in[i], 16 * (l + 1))
                eng.wait_ge(w_used, 2 * l + i + 1)
                eng.scalar_tensor_tensor(out=dst[:, l, :, :].rearrange("p k h -> p (k h)"),
                                         in0=stage[:, 2048 * i:2048 * (i + 1)], scalar=WS,
                                         in1=high[:, l, :, :].rearrange("p k h -> p (k h)"),
                                         op0=ALU.mult, op1=ALU.subtract).then_inc(w_split, 1)

            low_half(0, 0, w1l, w1h)
            low_half(0, 1, w2l, w2h)
            eng.wait_ge(const_ready, 2)
            for g in range(NG):
                eng.wait_ge(adj_in[g % 2], 16 * (g // 2 + 1))
                if g:
                    eng.wait_ge(init_chain, g + 1)
                eng.scalar_tensor_tensor(out=edge, in0=adji[:, g % 2, :, :], scalar=0.0,
                                         in1=ident[:, :].unsqueeze(1).to_broadcast([128, G, N]),
                                         op0=ALU.is_gt, op1=ALU.max).then_inc(adj_used, 1)
                eng.wait_ge(adj_used, g + 1)
                eng.tensor_scalar(mask[:, g, :, :], edge, 1.0, FAR, ALU.subtract, ALU.mult).then_inc(init_chain, 1)
            for l in range(1, L):
                low_half(l, 0, w1l, w1h)
                low_half(l, 1, w2l, w2h)
            eng.wait_ge(par_in, 16 * 10)
            eng.wait_ge(init_chain, NG + 1)

            def cols(s, slot, l, first=False):
                eng.wait_ge(x_ready, s + 1)
                for g in range(G):
                    for a in range(2):
                        if not first or g:
                            eng.wait_ge(cols_done, 2 * G * s + 2 * g + a - 1)
                        ins = eng.scalar_tensor_tensor(out=junk[:, a, :], in0=xs[:, slot, g, :], scalar=1.0,
                                                       in1=aw[:, l, a * D:(a + 1) * D], op0=ALU.mult, op1=ALU.mult,
                                                       accum_out=sij[:, a * G + g:a * G + g + 1])
                        ins.then_inc(cols_done, 1)

            def scores(s, slot, l):
                eng.wait_ge(cols_done, 2 * G * (s + 1))
                eng.wait_ge(spread_ready, s + 1)
                eng.scalar_tensor_tensor(out=v[:, :, :], in0=sp[:, :].rearrange("p (g n) -> p g n", g=G),
                                         scalar=ab[:, l:l + 1] if isinstance(l, int) else ab[:, bass.ds(l, 1)],
                                         in1=sij[:, 0:G].unsqueeze(2).to_broadcast([128, G, N]),
                                         op0=ALU.add, op1=ALU.add).then_inc(score_chain, 1)
                eng.wait_ge(score_chain, 3 * s + 1)
                eng.scalar_tensor_tensor(out=v[:, :, :], in0=v[:, :, :], scalar=SLOPE, in1=v[:, :, :],
                                         op0=ALU.mult, op1=ALU.max).then_inc(score_chain, 1)
                eng.wait_ge(score_chain, 3 * s + 2)
                eng.tensor_tensor(out=v[:, :, :], in0=v[:, :, :], in1=mask[:, slot, :, :], op=ALU.add)\
                   .then_inc(score_chain, 1)
                eng.wait_ge(score_chain, 3 * s + 3)
                eng.tensor_reduce(nm[:, :], v[:, :, :], AX.X, ALU.max, negate=True).then_inc(scores_ready, 1)

            def pt_copy(s):
                eng.wait_ge(exp_done, s + 1)
                eng.reciprocal(rinv[:, :], rs[:, :]).then_inc(rinv_ready, 1)
                eng.wait_ge(pt_ready, s + 1)
                eng.tensor_copy(pts[:, :, :].rearrange("p g n -> p (g n)"), sp[:, :]).then_inc(pt_copied, 1)

            def moments(zt, st, mv, ve, chain, base, var_ready):
                for g in range(G):
                    eng.wait_ge(chain, base + G + g)
                    eng.bn_stats(st[:, g, :], zt[:, g, :]).then_inc(chain, 1)
                    if g:
                        ins = eng.bn_aggr(mv[:, g - 1, :], st[:, g - 1, :])
                ins.then_inc(chain, 1)
                eng.wait_ge(chain, base + 2 * G + 1)
                eng.tensor_scalar(ve[:, 0:G - 1], mv[:, 0:G - 1, 1], EPS, None, ALU.add)
                eng.bn_aggr(mv[:, G - 1, :], st[:, G - 1, :]).then_inc(chain, 1)
                eng.wait_ge(chain, base + 2 * G + 2)
                eng.tensor_scalar(ve[:, G - 1:G], mv[:, G - 1:G, 1], EPS, None, ALU.add).then_inc(var_ready, 1)

            def norm1(s, slot, first=False):
                if not first:
                    eng.wait_ge(hb_ready, s)
                    eng.wait_ge(ht_ready, KD * s)
                eng.wait_ge(rinv_ready, s + 1)
                for g in range(G):
                    eng.wait_ge(agg_ready, G * s + g // 2 * 2 + 2)
                    eng.scalar_tensor_tensor(out=z[:, g, :], in0=pair(agg, g), scalar=rinv[:, g:g + 1],
                                             in1=xs[:, slot, g, :], op0=ALU.mult, op1=ALU.add).then_inc(ln1_chain, 1)
                moments(z, st1, mv1, ve1, ln1_chain, (2 * G + 2) * s, var1_ready)

            def norm1_end(s):
                eng.wait_ge(rstd1_ready, s + 1)
                for g in range(G):
                    ins = eng.tensor_scalar(z[:, g, :], z[:, g, :], mv1[:, g, 0:1], rstd1[:, g:g + 1],
                                            ALU.subtract, ALU.mult)
                ins.then_inc(z_ready, 1)

            def head_low(s):
                for k in range(KD):
                    eng.wait_ge(hth_done, KD * s + k + 1)
                    eng.tensor_tensor(out=ht[:, 1, k, :], in0=htf[:, k, :], in1=ht[:, 0, k, :], op=ALU.subtract)\
                       .then_inc(htl_done, 1)

            def gelu_low(t, m):
                eng.wait_ge(gh_done, KH * t + m + 1)
                eng.tensor_tensor(out=gt[:, 1, m, :], in0=g32[:, m % HB, :], in1=gt[:, 0, m, :], op=ALU.subtract)\
                   .then_inc(gl_done, 1)

            def norm2(t):
                eng.wait_ge(hb_ready, t + 1)
                for i in range(2):
                    eng.wait_ge(ff_ready, G * t + 2 * i + 2)
                    eng.scalar_tensor_tensor(out=z2[:, 2 * i:2 * i + 2, :].rearrange("p g d -> p (g d)"),
                                             in0=ff[i][:, :], scalar=1.0 / WS,
                                             in1=hb[:, t & 1, 2 * i:2 * i + 2, :].rearrange("p g d -> p (g d)"),
                                             op0=ALU.mult, op1=ALU.add).then_inc(ln2_chain, 2)
                moments(z2, st2, mv2, ve2, ln2_chain, (2 * G + 2) * t, var2_ready)

            def norm2_end(t):
                eng.wait_ge(rstd2_ready, t + 1)
                for g in range(G):
                    ins = eng.tensor_scalar(z2[:, g, :], z2[:, g, :], mv2[:, g, 0:1], rstd2[:, g:g + 1],
                                            ALU.subtract, ALU.mult)
                ins.then_inc(z2_ready, 1)

            cols(0, 0, 0, first=True)
            scores(0, 0, 0)
            pt_copy(0)
            norm1(0, 0, first=True)
            norm1_end(0)
            head_low(0)
            cols(1, 1, 0)
            scores(1, 1, 0)

            def step(t, first=False, more=2):
                gelu_low(t, 0)
                if not first:
                    if_wait = t - 1
                    if not (isinstance(t, int) and t == 1):
                        eng.wait_ge(x_stored, t - 1)
                    norm2(if_wait)
                for m in (1, 2):
                    gelu_low(t, m)
                if not first:
                    norm2_end(t - 1)
                for m in (3, 4):
                    gelu_low(t, m)
                if more >= 2:
                    cols(t + 2, (t + 2) & (NG - 1), layer(t + 2))
                gelu_low(t, 5)
                gelu_low(t, 6)
                gelu_low(t, 7)
                if more >= 1:
                    pt_copy(t + 1)
                    norm1(t + 1, (t + 1) & (NG - 1))
                if more >= 2:
                    scores(t + 2, (t + 2) & (NG - 1), layer(t + 2))
                if more >= 1:
                    norm1_end(t + 1)
                    head_low(t + 1)

            step(0, first=True)
            step(1)
            with eng.Fori(2, STEPS - 2) as t:
                step(t)
            step(STEPS - 2, more=1)
            step(STEPS - 1, more=0)
            eng.wait_ge(x_stored, STEPS - 1)
            norm2(STEPS - 1)
            norm2_end(STEPS - 1)


def wait(eng, sem, value):
    if not isinstance(value, int) or value > 0:
        eng.wait_ge(sem, value)


def other_networks(nc, xs, ident, half, bank, x, adj, w1g, a1g, w2g, bias, w3, b3_down, b3, attn3, out):
    ctx = ExitStack()
    with ctx:
        def sb(name, shape, dt=F32):
            return ctx.enter_context(nc.sbuf_tensor(name, shape, dt))

        sems = {}

        def sem(name):
            sems[name] = ctx.enter_context(nc.semaphore(name))
            return sems[name]

        wf = sb("wf", [128, KD, D])
        ab2 = sb("ab2", [128, 2, D])
        wa = sb("wa", [128, KD, 2])
        wm2 = sb("wm2", [128, 2, KD, D])
        wm = sb("wm", [128, KD, D])
        biasm = sb("biasm", [128, D])
        wb = sb("wb", [128, KD, D])
        wat = sb("wat", [128, KD, D])
        bb = sb("bb", [128, D])
        bc = sb("bc", [128, KD])
        identb = sb("identb", [128, 128], BF16)
        pick = sb("pick", [128, 4, 32], BF16)
        xin = sb("xin", [128, 2, G, D])
        adji = sb("adji2", [128, 2, G, N], I32)
        lab = sb("lab", [128, 4, G, N], BF16)
        r1 = sb("r1", [128, G, D])
        u1 = sb("u1", [128, G, D])
        u1t = sb("u1t", [128, KD, T])
        wh = sb("wh", [128, G, D])
        ec = sb("ec", [128, 2 * G])
        mkf = sb("mkf", [128, G, N], BF16)
        vf = sb("vf", [128, G, N])
        left = sb("left", [128, G, N])
        top = sb("top", [128, G, 2, 8])
        pause = sb("pause", [128, 1])
        nmf = sb("nmf", [128, G])
        rsf = sb("rsf", [128, G])
        rif = sb("rif", [128, G])
        ptf = sb("ptf", [128, G, N])
        negf = sb("negf", [128, G, D])
        posf = sb("posf", [128, G, D])
        u2 = sb("u2", [128, G, D])
        u2t = sb("u2t", [128, KD, T])
        labt = sb("labt", [128, T], BF16)
        hot = sb("hot", [128, 16, T], BF16)
        cnt = sb("cnt", [128, T])
        r3 = sb("r3", [128, G, D])
        u3 = sb("u3", [128, G, D])
        u3t = sb("u3t", [128, KD, T])
        hh = sb("hh", [128, G, D])
        hht = sb("hht", [128, KD, T])
        hat = sb("hat", [128, KD, T])
        mkb = sb("mkb", [128, G, N], BF16)
        vb = sb("vb", [128, G, N])
        nmb = sb("nmb", [128, G])
        rsb = sb("rsb", [128, G])
        rib = sb("rib", [128, G])
        ptb = sb("ptb", [128, G, N])
        negb = sb("negb", [128, G, D])
        posb = sb("posb", [128, G, D])
        y = sb("y", [128, G, D])

        class Norm:

            def __init__(self, name):
                self.st = sb(name + "_st", [128, G, 6])
                self.mv = sb(name + "_mv", [128, G, 2])
                self.ve = sb(name + "_ve", [128, G])
                self.rstd = sb(name + "_rstd", [128, G])
                self.chain = sem(name + "_chain")
                self.var_ready = sem(name + "_var_ready")
                self.rstd_ready = sem(name + "_rstd_ready")
                self.done = sem(name + "_done")

        n1, n2, n3, n4 = Norm("n1"), Norm("n2"), Norm("n3"), Norm("n4")

        fp, fs = bank[0:2], bank[2]
        mp = bank[3:5]
        bp, bs = bank[5:7], bank[7]

        def pair(banks, g):
            return banks[g // 2][:, (g % 2) * D:(g % 2 + 1) * D]

        def flat(t):
            return t[:, :, :].rearrange("p a b -> p (a b)")

        def half_of(t, i):
            return t[:, 2 * i:2 * i + 2, :].rearrange("p g d -> p (g d)")

        par_in = sem("par2_in")
        const_ready = sem("const2_ready")
        init_chain = sem("init2_chain")
        pick_chain = sem("pick_chain")
        wa_ready = sem("wa_ready")
        x_in = [sem(f"x2_in{i}") for i in range(2)]
        adj_in = [sem(f"adj2_in{i}") for i in range(2)]
        r1_ready = sem("r1_ready")
        lab_ready = sem("lab_ready")
        u1_turned, u1t_done = sem("u1_turned"), sem("u1t_done")
        wh_ready, wh_done = sem("wh_ready"), sem("wh_done")
        ec_ready, ec_done = sem("ec_ready"), sem("ec_done")
        fspread = sem("fspread")
        fchain = sem("fchain")
        fscores = sem("fscores")
        fexp = sem("fexp")
        fri = sem("fri")
        ftop_chain = sem("ftop_chain")
        ftop = sem("ftop")
        fturn, fturn_done = sem("fturn"), sem("fturn_done")
        fagg = sem("fagg")
        fneg, fpos, fexpn = sem("fneg"), sem("fpos"), sem("fexpn")
        fsum = sem("fsum")
        u2_raw = sem("u2_raw")
        lab_turned, labt_done = sem("lab_turned"), sem("labt_done")
        hot_ready = sem("hot_ready")
        cnt_ready, cnt_done = sem("cnt_ready"), sem("cnt_done")
        u2_turned, u2t_done = sem("u2_turned"), sem("u2t_done")
        mout = sem("mout")
        r3_ready = sem("r3_ready")
        u3_turned, u3t_done = sem("u3_turned"), sem("u3t_done")
        hht_ready, hht_done = sem("hht_ready"), sem("hht_done")
        hat_ready, hat_done = sem("hat_ready"), sem("hat_done")
        hh_ready, hh_done = sem("hh_ready"), sem("hh_done")
        bsc = sem("bsc")
        bchain = sem("bchain")
        bscores = sem("bscores")
        bexp = sem("bexp")
        bri = sem("bri")
        bturn, bturn_done = sem("bturn"), sem("bturn_done")
        bagg = sem("bagg")
        bneg, bpos, bexpn = sem("bneg"), sem("bpos"), sem("bexpn")
        bsum = sem("bsum")
        y_raw = sem("y_raw")
        out_done = sem("out_done")

        block = ctx.enter_context(nc.Block())

        def steps(eng, step):
            for i in range(-3, 1):
                step(i)
            with eng.Fori(1, NG - 3) as i:
                step(i)
            for i in range(NG - 3, NG + 1):
                step(i)

        def there(s):
            return not isinstance(s, int) or 0 <= s < NG

        @block.sync
        def _(eng):
            for dst, src in (
                (wf[:, :, :], w1g.rearrange("(k p) o -> p k o", p=128)),
                (ab2[:, :, :], a1g.partition_broadcast(128)),
                (wm2[:, :, :, :].rearrange("p w k o -> p (w k) o"), w2g.rearrange("(w k p) o -> p (w k) o", p=128, k=KD)),
                (wb[:, :, :], w3.rearrange("(k p) o -> p k o", p=128)),
                (wat[:, :, :], attn3.rearrange("(k p) o -> p k o", p=128)),
                (bb[:, :], b3.partition_broadcast(128)),
                (bc[:, :], b3_down),
            ):
                eng.dma_start(dst, src).then_inc(par_in, 16)
            eng.wait_ge(const_ready, 1)
            for c in range(4):
                eng.dma_start(biasm[32 * c:32 * c + 4, :], bias[c]).then_inc(par_in, 16)

            def load(s, b):
                eng.dma_start(adji[:, b, :, :], adj[s].rearrange("g i j -> i g j")).then_inc(adj_in[b], 16)
                eng.dma_start(xin[:, b, :, :], x[s].rearrange("g n d -> n g d")).then_inc(x_in[b], 16)

            def store(s):
                eng.wait_ge(n4.done, s + 1)
                eng.dma_start(out[s].rearrange("g n d -> n g d"), y[:, :, :]).then_inc(out_done, 16)

            load(0, 0)
            load(1, 1)
            for s in range(2, 6):
                eng.wait_ge(lab_ready, s - 1)
                eng.wait_ge(r1_ready, s - 1)
                load(s, s % 2)
            with eng.Fori(0, (NG - 6) // 2) as h:
                for b in range(2):
                    eng.wait_ge(lab_ready, 2 * h + 5 + b)
                    eng.wait_ge(r1_ready, 2 * h + 5 + b)
                    load(2 * h + 6 + b, b)
                    store(2 * h + b)
            for s in range(NG - 6, NG):
                store(s)
            eng.wait_ge(out_done, 16 * NG)

        @block.gpsimd
        def _(eng):
            eng.memset(biasm[:, :], 0.0).then_inc(const_ready, 1)
            eng.memset(pick[:, :, :], 0.0).then_inc(pick_chain, 1)
            eng.tensor_copy(identb[:, :], ident[:, :]).then_inc(const_ready, 1)
            eng.wait_ge(pick_chain, 1)
            eng.affine_select(out=pick[:, :, :], in_=pick[:, :, :], compare_op=ALU.not_equal, fill=1.0,
                              base=0, pattern=[[1, 4], [-1, 32]], channel_multiplier=0).then_inc(const_ready, 1)

            def root(n, s):
                if there(s):
                    eng.wait_ge(n.var_ready, s + 1)
                    eng.tensor_tensor(out=n.rstd[:, :], in0=n.ve[:, :], in1=half[:, :], op=ALU.pow)\
                       .then_inc(n.rstd_ready, 1)

            def enter(s, b):
                if there(s):
                    eng.wait_ge(adj_in[b], 16 * (s // 2 + 1) if isinstance(s, int) else ((s >> 1) + 1) * 16)
                    wait(eng, n1.done, s)
                    wait(eng, bscores, s - 3)
                    eng.tensor_copy(lab[:, s & 3, :, :], adji[:, b, :, :]).then_inc(lab_ready, 1)
                    eng.wait_ge(x_in[b], 16 * (s // 2 + 1) if isinstance(s, int) else ((s >> 1) + 1) * 16)
                    eng.tensor_tensor(out=r1[:, :, :], in0=xin[:, b, :, :], in1=xs[:, s, :, :], op=ALU.add)\
                       .then_inc(r1_ready, 1)

            def add_pos(s, total, total_ready, pos, pos_ready, raw):
                if there(s):
                    eng.wait_ge(total_ready, s + 1)
                    eng.wait_ge(pos_ready, s + 1)
                    eng.tensor_tensor(out=total[:, :, :], in0=total[:, :, :], in1=pos[:, :, :], op=ALU.add)\
                       .then_inc(raw, 1)

            def step(i, b):
                root(n2, i + 1)
                root(n4, i - 1)
                enter(i + 3, b)
                root(n3, i + 1)
                root(n1, i + 3)
                add_pos(i + 2, u2, fsum, posf, fpos, u2_raw)
                add_pos(i, y, bsum, posb, bpos, y_raw)

            for i in range(-3, 1):
                step(i, (i + 3) % 2)
            with eng.Fori(0, (NG - 4) // 2) as h:
                step(2 * h + 1, 0)
                step(2 * h + 2, 1)
            for i in range(NG - 3, NG + 1):
                step(i, 0)

        @block.scalar
        def _(eng):
            eng.wait_ge(par_in, 16 * 11)

            def banks_out(s, banks, ready, dst, done, bias_col=None):
                if there(s):
                    for k in range(2):
                        eng.wait_ge(ready, 2 * s + k + 1)
                        if bias_col is None:
                            eng.activation(dst(k), banks[k][:, :], ACT.Copy).then_inc(done, 1)
                        else:
                            eng.activation(dst(k), banks[k][:, :], ACT.Identity, bias=bias_col[:, k:k + 1])\
                               .then_inc(done, 1)

            def one_out(s, src, ready, dst, done):
                if there(s):
                    eng.wait_ge(ready, s + 1)
                    eng.activation(dst, src, ACT.Copy).then_inc(done, 1)

            def exps(s, vt, nm, rs, scores_ready, done):
                if there(s):
                    eng.wait_ge(scores_ready, s + 1)
                    for g in range(G):
                        ins = eng.activation(vt[:, g, :], vt[:, g, :], ACT.Exp, bias=nm[:, g:g + 1],
                                             accum_out=rs[:, g:g + 1])
                    ins.then_inc(done, 1)

            def elu(s, banks, agg_ready, ri, ri_ready, pos, pos_ready, neg, neg_ready, expn, raw):
                if there(s):
                    eng.wait_ge(ri_ready, s + 1)
                    wait(eng, raw, s)
                    for g in range(G):
                        eng.wait_ge(agg_ready, G * s + g // 2 * 2 + 2)
                        eng.wait_ge(neg_ready, 2 * s + g // 2 + 1)
                        ins = eng.activation(pos[:, g, :], pair(banks, g), ACT.Relu, scale=ri[:, g:g + 1])
                    ins.then_inc(pos_ready, 1)
                    eng.activation(flat(neg), flat(neg), ACT.Exp).then_inc(expn, 1)

            def step(i):
                banks_out(i + 2, fp, u1_turned, lambda k: u1t[:, k, :], u1t_done)
                one_out(i + 1, mp[0][:, :].bitcast(BF16)[:, 0:T], lab_turned, labt[:, :], labt_done)
                banks_out(i, bp, u3_turned, lambda k: u3t[:, k, :], u3t_done)
                banks_out(i + 2, fp, wh_ready, lambda k: half_of(wh, k), wh_done)
                one_out(i + 2, fs[:, 0:2 * G], ec_ready, ec[:, :], ec_done)
                banks_out(i, bp, hht_ready, lambda k: hht[:, k, :], hht_done, bc)
                one_out(i + 1, mp[1][:, :], cnt_ready, cnt[:, :], cnt_done)
                banks_out(i + 1, mp, u2_turned, lambda k: u2t[:, k, :], u2t_done)
                banks_out(i, bp, hat_ready, lambda k: hat[:, k, :], hat_done)
                exps(i + 2, vf, nmf, rsf, fscores, fexp)
                exps(i, vb, nmb, rsb, bscores, bexp)
                one_out(i + 2, fs[:, :], fturn, flat(ptf), fturn_done)
                elu(i + 2, fp, fagg, rif, fri, posf, fpos, negf, fneg, fexpn, u2_raw)
                one_out(i, bs[:, :], bturn, flat(ptb), bturn_done)
                elu(i, bp, bagg, rib, bri, posb, bpos, negb, bneg, bexpn, y_raw)

            steps(eng, step)

        @block.tensor
        def _(eng):
            eng.wait_ge(par_in, 16 * 11)
            eng.wait_ge(const_ready, 3)
            eng.wait_ge(wa_ready, 5)

            def turn_features(s, src, src_ready, banks, turned, bank_free, free_count):
                if there(s):
                    eng.wait_ge(src_ready, s + 1)
                    wait(eng, bank_free, free_count)
                    for k in range(KD):
                        for g in range(G):
                            ins = eng.transpose(banks[k][:, g * N:(g + 1) * N], src[:, g, k * 128:(k + 1) * 128],
                                                ident[:, :])
                        ins.then_inc(turned, 1)

            def turn_probs(s, src, src_ready, bank_, turned):
                if there(s):
                    eng.wait_ge(src_ready, s + 1)
                    for g in range(G):
                        ins = eng.transpose(bank_[:, g * N:(g + 1) * N], src[:, g, :], ident[:, :])
                    ins.then_inc(turned, 1)

            def turn_labels(s):
                if there(s):
                    eng.wait_ge(lab_ready, s + 1)
                    wait(eng, r3_ready, 2 * s)
                    for g in range(G):
                        ins = eng.transpose(mp[0][:, :].bitcast(BF16)[:, g * N:(g + 1) * N],
                                            lab[:, s & 3, g, :], identb[:, :])
                    ins.then_inc(lab_turned, 1)

            def project(s):
                if there(s):
                    eng.wait_ge(u1t_done, 2 * s + 2)
                    for g in range(G):
                        for k in range(KD):
                            ins = eng.matmul(pair(fp, g), u1t[:, k, g * N:(g + 1) * N], wf[:, k, :],
                                             start=(k == 0), stop=(k == KD - 1))
                        if g % 2:
                            ins.then_inc(wh_ready, 1)
                    wait(eng, fturn_done, s)
                    for g in range(G):
                        for k in range(KD):
                            ins = eng.matmul(fs[:, 2 * g:2 * g + 2], u1t[:, k, g * N:(g + 1) * N], wa[:, k, :],
                                             start=(k == 0), stop=(k == KD - 1))
                    ins.then_inc(ec_ready, 1)

            def spread(s):
                if there(s):
                    eng.wait_ge(ec_done, s + 1)
                    for g in range(G):
                        ins = eng.matmul(fs[:, g * N:(g + 1) * N],
                                         ec[:, 2 * g + 1:2 * g + 2].to_broadcast([128, 128]), ident[:, :],
                                         start=True, stop=True)
                    ins.then_inc(fspread, 1)

            def gather(s, pt, pt_done, feats, feats_done, feats_count, banks, ready):
                if there(s):
                    eng.wait_ge(pt_done, s + 1)
                    eng.wait_ge(feats_done, feats_count)
                    for g in range(G):
                        eng.matmul(pair(banks, g), pt[:, g, :], feats[:, g, :], start=True, stop=True)\
                           .then_inc(ready, 1)

            def count(s):
                if there(s):
                    for q in range(4):
                        eng.wait_ge(hot_ready, 4 * s + q + 1)
                        for c in range(4):
                            ins = eng.matmul(mp[1][32 * c:32 * c + 32, :], pick[:, q, :], hot[:, 4 * q + c, :],
                                             start=(q == 0), stop=(q == 3), tile_position=(0, 32 * c))
                    ins.then_inc(cnt_ready, 1)

            def mid(s):
                if there(s):
                    eng.wait_ge(u2t_done, 2 * s + 2)
                    eng.wait_ge(cnt_done, s + 1)
                    for g in range(G):
                        for k in range(KD):
                            eng.matmul(pair(mp, g), u2t[:, k, g * N:(g + 1) * N], wm[:, k, :],
                                       start=(k == 0), stop=False)
                        ins = eng.matmul(pair(mp, g), cnt[:, g * N:(g + 1) * N], biasm[:, :], start=False, stop=True)
                        if g % 2:
                            ins.then_inc(mout, 1)

            def across(s, w, src, src_done, done):
                if there(s):
                    eng.wait_ge(src_done, 2 * s + 2)
                    for o in range(KD):
                        for k in range(KD):
                            ins = eng.matmul(bp[o][:, :], w[:, k, o * 128:(o + 1) * 128], src[:, k, :],
                                             start=(k == 0), stop=(k == KD - 1))
                        ins.then_inc(done, 1)

            def along(s):
                if there(s):
                    eng.wait_ge(hat_done, 2 * s + 2)
                    for g in range(G):
                        for k in range(KD):
                            ins = eng.matmul(pair(bp, g), u3t[:, k, g * N:(g + 1) * N], wb[:, k, :],
                                             start=(k == 0), stop=(k == KD - 1))
                        if g % 2:
                            ins.then_inc(hh_ready, 1)

            def back_scores(s):
                if there(s):
                    wait(eng, bturn_done, s)
                    for g in range(G):
                        for k in range(KD):
                            ins = eng.matmul(bs[:, g * N:(g + 1) * N], hat[:, k, g * N:(g + 1) * N],
                                             hht[:, k, g * N:(g + 1) * N], start=(k == 0), stop=(k == KD - 1))
                    ins.then_inc(bsc, 1)

            def step(i):
                f, m, b = i + 2, i + 1, i
                turn_features(f, u1, n1.done, fp, u1_turned, fpos, f)
                turn_labels(m)
                turn_features(b, u3, n3.done, bp, u3_turned, bpos, b)
                project(f)
                across(b, wb, u3t, u3t_done, hht_ready)
                count(m)
                spread(f)
                if there(m):
                    eng.wait_ge(labt_done, m + 1)
                    eng.wait_ge(cnt_done, m + 1)
                turn_features(m, u2, n2.done, mp, u2_turned, r3_ready, 2 * m)
                across(b, wat, hht, hht_done, hat_ready)
                mid(m)
                along(b)
                back_scores(b)
                turn_probs(f, vf, ftop, fs, fturn)
                gather(f, ptf, fturn_done, wh, wh_done, 2 * f + 2, fp, fagg)
                turn_probs(b, vb, bexp, bs, bturn)
                gather(b, ptb, bturn_done, hh, hh_done, 2 * b + 2, bp, bagg)

            steps(eng, step)

        @block.vector
        def _(eng):
            eng.wait_ge(par_in, 16 * 11)
            eng.tensor_tensor(out=flat(wm), in0=wm2[:, 0, :, :].rearrange("p k o -> p (k o)"),
                              in1=wm2[:, 1, :, :].rearrange("p k o -> p (k o)"), op=ALU.add).then_inc(wa_ready, 1)
            for k in range(KD):
                for a in range(2):
                    eng.scalar_tensor_tensor(out=negf[:, 2 * k + a, :], in0=wf[:, k, :], scalar=1.0,
                                             in1=ab2[:, a, :], op0=ALU.mult, op1=ALU.mult,
                                             accum_out=wa[:, k, a:a + 1]).then_inc(wa_ready, 1)
            eng.wait_ge(wa_ready, 5)

            def moments(s, n, src, ready):
                if there(s):
                    eng.wait_ge(ready, s + 1)
                    base = (G + 2) * s
                    for g in range(G):
                        if g:
                            eng.wait_ge(n.chain, base + g)
                        eng.bn_stats(n.st[:, g, :], src[:, g, :]).then_inc(n.chain, 1)
                        if g:
                            ins = eng.bn_aggr(n.mv[:, g - 1, :], n.st[:, g - 1, :])
                    ins.then_inc(n.chain, 1)
                    eng.wait_ge(n.chain, base + G + 1)
                    eng.tensor_scalar(n.ve[:, 0:G - 1], n.mv[:, 0:G - 1, 1], EPS, None, ALU.add)
                    eng.bn_aggr(n.mv[:, G - 1, :], n.st[:, G - 1, :]).then_inc(n.chain, 1)
                    eng.wait_ge(n.chain, base + G + 2)
                    eng.tensor_scalar(n.ve[:, G - 1:G], n.mv[:, G - 1:G, 1], EPS, None, ALU.add)\
                       .then_inc(n.var_ready, 1)

            def normed(s, n, src, dst, readers=()):
                if there(s):
                    eng.wait_ge(n.rstd_ready, s + 1)
                    for reader, count in readers:
                        wait(eng, reader, count)
                    for g in range(G):
                        ins = eng.tensor_scalar(dst[:, g, :], src[:, g, :], n.mv[:, g, 0:1], n.rstd[:, g:g + 1],
                                                ALU.subtract, ALU.mult)
                    ins.then_inc(n.done, 1)

            def hots(s):
                if there(s):
                    eng.wait_ge(labt_done, s + 1)
                    wait(eng, cnt_ready, s)
                    for l in range(16):
                        ins = eng.tensor_scalar(hot[:, l, :], labt[:, :], float(l), None, ALU.is_equal)
                        if l % 4 == 3:
                            ins.then_inc(hot_ready, 1)

            def front_scores(s):
                if there(s):
                    eng.tensor_scalar(mkf[:, :, :], lab[:, s & 3, :, :], 0.0, -3e38, ALU.is_equal, ALU.mult)\
                       .then_inc(fchain, 1)
                    eng.wait_ge(fspread, s + 1)
                    wait(eng, fturn, s)
                    src = ec[:, :].rearrange("p (g c) -> p g c", c=2)[:, :, 0:1].to_broadcast([128, G, N])
                    eng.tensor_tensor(out=vf[:, :, :], in0=fs[:, :].rearrange("p (g n) -> p g n", g=G),
                                      in1=src, op=ALU.add).then_inc(fchain, 1)
                    eng.wait_ge(fchain, 4 * s + 2)
                    eng.scalar_tensor_tensor(out=vf[:, :, :], in0=vf[:, :, :], scalar=SLOPE, in1=vf[:, :, :],
                                             op0=ALU.mult, op1=ALU.max).then_inc(fchain, 1)
                    eng.wait_ge(fchain, 4 * s + 3)
                    eng.scalar_tensor_tensor(out=vf[:, :, :], in0=mkf[:, :, :], scalar=FAR / 3e38, in1=vf[:, :, :],
                                             op0=ALU.mult, op1=ALU.add).then_inc(fchain, 1)
                    eng.wait_ge(fchain, 4 * s + 4)
                    eng.tensor_reduce(nmf[:, :], vf[:, :, :], AX.X, ALU.max, negate=True).then_inc(fscores, 1)

            def largest(s):
                if there(s):
                    eng.wait_ge(fexp, s + 1)
                    eng.reciprocal(rif[:, :], rsf[:, :]).then_inc(fri, 1)
                    for g in range(G):
                        ins = eng.max(top[:, g, 0, :], vf[:, g, :])
                    ins.then_inc(ftop_chain, 1)
                    eng.wait_ge(ftop_chain, 5 * s + 1)
                    eng.memset(pause[:, 0:1], 0.0).then_inc(ftop_chain, 1)
                    for g in range(G):
                        ins = eng.match_replace(left[:, g, :], top[:, g, 0, :], vf[:, g, :], -1.0)
                    ins.then_inc(ftop_chain, 1)
                    eng.wait_ge(ftop_chain, 5 * s + 3)
                    eng.memset(pause[:, 0:1], 0.0).then_inc(ftop_chain, 1)
                    for g in range(G):
                        ins = eng.max(top[:, g, 1, :], left[:, g, :])
                    ins.then_inc(ftop_chain, 1)
                    eng.wait_ge(ftop_chain, 5 * s + 5)
                    for g in range(G):
                        ins = eng.scalar_tensor_tensor(out=vf[:, g, :], in0=vf[:, g, :], scalar=top[:, g, 1, 7:8],
                                                       in1=vf[:, g, :], op0=ALU.is_ge, op1=ALU.mult)
                    ins.then_inc(ftop, 1)

            def negatives(s, banks, agg_ready, ri, ri_ready, neg, neg_ready):
                if there(s):
                    eng.wait_ge(ri_ready, s + 1)
                    for g in range(G):
                        eng.wait_ge(agg_ready, G * s + g // 2 * 2 + 2)
                        ins = eng.tensor_scalar(neg[:, g, :], pair(banks, g), ri[:, g:g + 1], 0.0, ALU.mult, ALU.min)
                        if g % 2:
                            ins.then_inc(neg_ready, 1)

            def less_one(s, neg, expn, base, dst, sum_ready, readers=()):
                if there(s):
                    eng.wait_ge(expn, s + 1)
                    for reader, count in readers:
                        wait(eng, reader, count)
                    eng.scalar_tensor_tensor(out=flat(dst), in0=flat(neg), scalar=-1.0, in1=flat(base),
                                             op0=ALU.add, op1=ALU.add).then_inc(sum_ready, 1)

            def mid_sum(s):
                if there(s):
                    wait(eng, n3.done, s)
                    for k in range(2):
                        eng.wait_ge(mout, 2 * s + k + 1)
                        eng.scalar_tensor_tensor(out=half_of(r3, k), in0=half_of(u2, k), scalar=2.0,
                                                 in1=mp[k][:, :], op0=ALU.mult, op1=ALU.add).then_inc(r3_ready, 1)

            def add_bias(s):
                if there(s):
                    for k in range(2):
                        eng.wait_ge(hh_ready, 2 * s + k + 1)
                        eng.tensor_tensor(out=hh[:, 2 * k:2 * k + 2, :],
                                          in0=bp[k][:, :].rearrange("p (g d) -> p g d", g=2),
                                          in1=bb[:, :].unsqueeze(1).to_broadcast([128, 2, D]), op=ALU.add)\
                           .then_inc(hh_done, 1)

            def back_softmax(s):
                if there(s):
                    eng.tensor_scalar(mkb[:, :, :], lab[:, s & 3, :, :], 0.0, -3e38, ALU.is_equal, ALU.mult)\
                       .then_inc(bchain, 1)
                    eng.wait_ge(bchain, 2 * s + 1)
                    wait(eng, bturn, s)
                    eng.wait_ge(bsc, s + 1)
                    eng.tensor_tensor(out=vb[:, :, :], in0=mkb[:, :, :],
                                      in1=bs[:, :].rearrange("p (g n) -> p g n", g=G), op=ALU.add).then_inc(bchain, 1)
                    eng.wait_ge(bchain, 2 * s + 2)
                    eng.tensor_reduce(nmb[:, :], vb[:, :, :], AX.X, ALU.max, negate=True).then_inc(bscores, 1)

            def back_recip(s):
                if there(s):
                    eng.wait_ge(bexp, s + 1)
                    eng.reciprocal(rib[:, :], rsb[:, :]).then_inc(bri, 1)

            def step(i):
                f, m, b = i + 2, i + 1, i
                normed(b, n3, r3, u3, [(bsum, b)])
                normed(f, n1, r1, u1, [(fsum, f), (u1_turned, 2 * f)])
                moments(m, n2, u2, u2_raw)
                normed(m, n2, u2, u2)
                hots(m)
                moments(b - 1, n4, y, y_raw)
                normed(b - 1, n4, y, y)
                moments(f + 1, n1, r1, r1_ready)
                front_scores(f)
                largest(f)
                if there(m):
                    mid_sum(m)
                    eng.wait_ge(r3_ready, 2 * m + 2)
                moments(m, n3, r3, n2.done)
                add_bias(b)
                back_softmax(b)
                back_recip(b)
                negatives(f, fp, fagg, rif, fri, negf, fneg)
                less_one(f, negf, fexpn, u1, u2, fsum, [(u2_turned, 2 * f), (r3_ready, 2 * f)])
                negatives(b, bp, bagg, rib, bri, negb, bneg)
                less_one(b, negb, bexpn, u3, y, bsum, [(out_done, 16 * b)])

            steps(eng, step)


def layer(s):
    return s // NG if isinstance(s, int) else (s >> (NG.bit_length() - 1)).with_bounds(min_val=0, max_val=L - 1)


def reuse(m):
    held = [i for i in range(KH) if i % HB == m % HB]
    return m - HB + 1 if m >= HB else held[-1] - KH + 1


def build(nc, x, adj, first, others, out):
    with (
        nc.sbuf_tensor("xs", [128, NG, G, D], F32) as xs,
        nc.sbuf_tensor("ident", [128, 128], F32) as ident,
        nc.sbuf_tensor("half", [128, G], F32) as half,
        ExitStack() as ctx,
    ):
        bank = [ctx.enter_context(nc.psum_tensor(f"bank{i}", [128, T], F32)) for i in range(8)]
        first_network(nc, xs, ident, half, bank, x, adj, *first)
        other_networks(nc, xs, ident, half, bank, x, adj, *others, out)


def kernel(**inputs):
    import numpy as np
    import concourse.bacc as bacc
    from concourse.bass_utils import run_bass_kernel_spmd as run

    nc = bacc.Bacc("TRN2", target_bir_lowering=False, num_devices=1)
    arrays = {}

    def give(name, shape=None, order=None, as_name=None):
        a = np.asarray(inputs[name])
        if shape:
            a = a.reshape(shape)
        if order:
            a = a.transpose(order)
        name = "in_" + (as_name or name)
        arrays[name] = np.ascontiguousarray(a)
        return nc.dram_tensor(name, a.shape, mybir.dt.from_np(a.dtype), kind="ExternalInput").ap()

    def down(name):
        return give(name, (L, -1, 128), (2, 0, 1), name + "_down")

    x = give("x", (NG, G, N, D))
    adj = give("adj", (NG, G, N, N))
    first = [give("L0_gnn_attn_w"), give("L0_gnn_attn_b"), give("L0_gnn_W1"), down("L0_gnn_b1"), give("L0_gnn_W2"),
             give("L0_gnn_b2"), give("L0_gnn_g1"), give("L0_gnn_beta1"), give("L0_gnn_g2"), give("L0_gnn_beta2"),
             down("L0_gnn_g1"), down("L0_gnn_beta1")]
    others = [give("L1_gnn_W"), give("L1_gnn_a", (2, D)),
              give("L2_gnn_weights", (2, D, D), (0, 2, 1)).rearrange("w i o -> (w i) o"),
              give("L2_gnn_bias", (4, 4, D), (1, 0, 2)),
              give("L3_gnn_W", None, (1, 0)), give("L3_gnn_b", (KD, 128), (1, 0), "b3_down"), give("L3_gnn_b"),
              give("L3_gnn_attn")]
    out = nc.dram_tensor("out", (NG, G, N, D), F32, kind="ExternalOutput").ap()
    build(nc, x, adj, first, others, out)
    r = run(nc, [arrays], core_ids=[0])
    return r.results[0]["out"].reshape(B, N, D)
```

```python
import concourse.bass as bass
from concourse import mybir
from contextlib import ExitStack

F32, F16, BF16, I32 = mybir.dt.float32, mybir.dt.float16, mybir.dt.bfloat16, mybir.dt.int32
ALU, ACT, AX = mybir.AluOpType, mybir.ActivationFunctionType, mybir.AxisListType

B, N, D = 64, 128, 256
G = 4
NG = B // G
T = G * N
L = 3
KD = D // 128
H = 4 * D
KH = H // 128
STEPS = L * NG
EPS = 1e-5
SLOPE = 0.2
FAR = 9e15
WS = 64.0
HB = 3
PT_AT = 2
AGG_AT = 6


def first_network(nc, xs, ident, half, bank, x, adj, attn_w, attn_b, w1, b1_down, w2, b2, g1, beta1, g2, beta2, g1_down, beta1_down):
    ctx = ExitStack()
    with ctx:
        def sb(name, shape, dt=F32):
            return ctx.enter_context(nc.sbuf_tensor(name, shape, dt))

        def sem(name):
            return ctx.enter_context(nc.semaphore(name))

        mask = sb("mask", [128, NG, G, N], BF16)
        w1h = sb("w1h", [128, L, KD, H], F16)
        w1l = sb("w1l", [128, L, KD, H], F16)
        w2h = sb("w2h", [128, L, KH, D], F16)
        w2l = sb("w2l", [128, L, KH, D], F16)
        aw = sb("aw", [128, L, 2 * D])
        ab = sb("ab", [128, L])
        g1b = sb("g1b", [128, L, D])
        betab = sb("betab", [128, L, D])
        g2b = sb("g2b", [128, L, D])
        beta2b = sb("beta2b", [128, L, D])
        b1c = sb("b1c", [128, L, KH])
        g1c = sb("g1c", [128, L, KD])
        beta1c = sb("beta1c", [128, L, KD])
        gt = sb("gt", [128, 2, KH, T], F16)
        stage = gt[:, :, :, :].rearrange("p a k t -> p (a k t)").bitcast(F32)
        ht = sb("ht", [128, 2, KD, T], F16)
        g32 = sb("g32", [128, HB, T])
        z = sb("z", [128, G, D])
        z2 = sb("z2", [128, G, D])
        hb = sb("hb", [128, 2, G, D])
        v = sb("v", [128, G, N])
        pts = sb("pts", [128, G, N])
        junk = sb("junk", [128, 2, D])
        junk_b2 = hb[:, 0, 0:3, :]
        adji = z[:, :, :].rearrange("p g d -> p (g d)").rearrange("p (b g n) -> p b g n", b=2, g=G).bitcast(I32)
        edge = z2[:, 0:2, :].rearrange("p a (b n) -> p (a b) n", b=2)
        sij = sb("sij", [128, 2 * G])
        nm = sb("nm", [128, G])
        rs = sb("rs", [128, G])
        rinv = sb("rinv", [128, G])
        st1 = sb("st1", [128, G, 6])
        mv1 = sb("mv1", [128, G, 2])
        ve1 = sb("ve1", [128, G])
        rstd1 = sb("rstd1", [128, G])
        st2 = sb("st2", [128, G, 6])
        mv2 = sb("mv2", [128, G, 2])
        ve2 = sb("ve2", [128, G])
        rstd2 = sb("rstd2", [128, G])

        hid = bank[0:HB]
        ff = bank[3:5]
        agg = bank[5:7]
        sp = bank[7]

        def pair(banks, g):
            return banks[g // 2][:, (g % 2) * D:(g % 2 + 1) * D]

        par_in = sem("par_in")
        w_in = [sem(f"w_in{i}") for i in range(2)]
        x_in = [sem(f"x_in{i}") for i in range(2)]
        adj_in = [sem(f"adj_in{i}") for i in range(2)]
        adj_used = sem("adj_used")
        w_used = sem("w_used")
        shift_ready = sem("shift_ready")
        b1_ready = sem("b1_ready")
        g1c_ready = sem("g1c_ready")
        w_split = sem("w_split")
        const_ready = sem("const_ready")
        init_chain = sem("init_chain")
        x_ready = sem("x_ready")
        cols_done = sem("cols_done")
        spread_ready = sem("spread_ready")
        scores_ready = sem("scores_ready")
        score_chain = sem("score_chain")
        exp_done = sem("exp_done")
        rinv_ready = sem("rinv_ready")
        pt_ready = sem("pt_ready")
        pt_copied = sem("pt_copied")
        agg_ready = sem("agg_ready")
        ln1_chain = sem("ln1_chain")
        var1_ready = sem("var1_ready")
        rstd1_ready = sem("rstd1_ready")
        z_ready = sem("z_ready")
        ht_ready = sem("ht_ready")
        hth_done = sem("hth_done")
        htl_done = sem("htl_done")
        hb_chain = sem("hb_chain")
        hb_ready = sem("hb_ready")
        hid_ready = sem("hid_ready")
        gelu_done = sem("gelu_done")
        gh_done = sem("gh_done")
        gl_done = sem("gl_done")
        ff_ready = sem("ff_ready")
        ln2_chain = sem("ln2_chain")
        var2_ready = sem("var2_ready")
        rstd2_ready = sem("rstd2_ready")
        z2_ready = sem("z2_ready")
        x_chain = sem("x_chain")
        x_stored = sem("x_stored")

        block = ctx.enter_context(nc.Block())

        @block.sync
        def _(eng):
            def load_w(l):
                eng.dma_start(stage[:, 0:2048].rearrange("p (k h) -> p k h", k=KD),
                              w1[l].rearrange("(k p) h -> p k h", p=128)).then_inc(w_in[0], 16)
                eng.dma_start(stage[:, 2048:4096].rearrange("p (k d) -> p k d", k=KH),
                              w2[l].rearrange("(k p) d -> p k d", p=128)).then_inc(w_in[1], 16)

            def load_adj(g, b):
                eng.dma_start(adji[:, b, :, :], adj[g].rearrange("g i j -> i g j")).then_inc(adj_in[b], 16)

            def load_x(g, b):
                eng.dma_start(xs[:, g, :, :], x[g].rearrange("g n d -> n g d")).then_inc(x_in[b], 16)

            load_w(0)
            load_adj(0, 0)
            load_adj(1, 1)
            load_x(0, 0)
            load_x(1, 1)
            for g in range(2, NG):
                eng.wait_ge(adj_used, g - 1)
                load_adj(g, g % 2)
            for l in range(1, L):
                eng.wait_ge(w_used, (KD + 1) * l)
                eng.wait_ge(w_split, (KD + 1) * l)
                eng.wait_ge(shift_ready, l)
                load_w(l)
            for g in range(NG):
                eng.wait_ge(x_in[g % 2], 16 * (g // 2 + 1))
                eng.sem_inc(x_ready, 1)
                if g + 2 < NG:
                    load_x(g + 2, g % 2)
            with eng.Fori(NG, STEPS) as s:
                eng.wait_ge(x_stored, s - (NG - 1))
                eng.sem_inc(x_ready, 1)

        @block.gpsimd
        def _(eng):
            eng.memset(ident[:, :], 0.0).then_inc(init_chain, 1)
            eng.memset(half[:, :], -0.5).then_inc(const_ready, 1)
            eng.wait_ge(init_chain, 1)
            eng.affine_select(out=ident[:, :], in_=ident[:, :], compare_op=ALU.not_equal, fill=1.0,
                              base=0, pattern=[[-1, 128]], channel_multiplier=1).then_inc(const_ready, 1)
            for tile, src in ((aw, attn_w), (g1b, g1), (betab, beta1), (junk_b2, b2), (g2b, g2), (beta2b, beta2)):
                eng.dma_start(tile[:, :, :], src.partition_broadcast(128)).then_inc(par_in, 16)
            eng.dma_start(ab[:, :], attn_b.partition_broadcast(128)).then_inc(par_in, 16)
            for tile, src in ((b1c, b1_down), (g1c, g1_down), (beta1c, beta1_down)):
                eng.dma_start(tile[:, :, :], src).then_inc(par_in, 16)
            eng.wait_ge(par_in, 16 * 10)
            eng.tensor_tensor(out=betab[:, :, :], in0=betab[:, :, :], in1=junk_b2[:, :, :], op=ALU.add)\
               .then_inc(hb_chain, 1)

            def wide(t, l):
                return t[:, l, :].unsqueeze(1).to_broadcast([128, G, D])

            def root(var_ready, rstd_ready, ve, rstd, s):
                eng.wait_ge(var_ready, s + 1)
                eng.tensor_tensor(out=rstd[:, :], in0=ve[:, :], in1=half[:, :], op=ALU.pow).then_inc(rstd_ready, 1)

            def gain1(s, l):
                eng.wait_ge(z_ready, s + 1)
                eng.tensor_tensor(out=hb[:, s & 1, :, :], in0=z[:, :, :], in1=wide(g1b, l), op=ALU.mult)\
                   .then_inc(hb_chain, 1)
                eng.wait_ge(hb_chain, s + 2)
                eng.tensor_tensor(out=hb[:, s & 1, :, :], in0=hb[:, s & 1, :, :], in1=wide(betab, l), op=ALU.add)\
                   .then_inc(hb_ready, 1)

            def gain2(s, slot, l):
                eng.wait_ge(z2_ready, s + 1)
                eng.tensor_tensor(out=xs[:, slot, :, :], in0=z2[:, :, :], in1=wide(g2b, l), op=ALU.mult)\
                   .then_inc(x_chain, 1)
                eng.wait_ge(x_chain, s + 1)
                eng.tensor_tensor(out=xs[:, slot, :, :], in0=xs[:, slot, :, :], in1=wide(beta2b, l), op=ALU.add)\
                   .then_inc(x_stored, 1)

            root(var1_ready, rstd1_ready, ve1, rstd1, 0)
            gain1(0, 0)

            def step(t, first=False, last=False):
                if not first:
                    u = t - 1
                    root(var2_ready, rstd2_ready, ve2, rstd2, u)
                    gain2(u, u & (NG - 1), layer(u))
                if not last:
                    s = t + 1
                    root(var1_ready, rstd1_ready, ve1, rstd1, s)
                    gain1(s, layer(s))

            step(0, first=True)
            with eng.Fori(1, STEPS - 1) as t:
                step(t)
            step(STEPS - 1, last=True)
            root(var2_ready, rstd2_ready, ve2, rstd2, STEPS - 1)
            gain2(STEPS - 1, NG - 1, L - 1)

        @block.scalar
        def _(eng):
            eng.wait_ge(g1c_ready, 1)
            for l in range(L):
                eng.wait_ge(w_in[0], 16 * (l + 1))
                for k in range(KD):
                    eng.activation(w1h[:, l, k, :], stage[:, H * k:H * (k + 1)], ACT.Copy,
                                   scale=g1c[:, l, k:k + 1]).then_inc(w_used, 1)
                eng.wait_ge(w_in[1], 16 * (l + 1))
                eng.activation(w2h[:, l, :, :].rearrange("p k h -> p (k h)"), stage[:, KD * H:2 * KD * H],
                               ACT.Copy, scale=WS).then_inc(w_used, 1)

            def exps(s):
                eng.wait_ge(scores_ready, s + 1)
                for g in range(G):
                    ins = eng.activation(v[:, g, :], v[:, g, :], ACT.Exp, bias=nm[:, g:g + 1],
                                         accum_out=rs[:, g:g + 1])
                ins.then_inc(exp_done, 1)

            def heads(s):
                for k in range(KD):
                    eng.wait_ge(ht_ready, KD * s + k + 1)
                    eng.activation(ht[:, 0, k, :], agg[k][:, :], ACT.Copy).then_inc(hth_done, 1)

            def pt_copy(s):
                eng.wait_ge(pt_ready, s + 1)
                eng.activation(pts[:, :, :].rearrange("p g n -> p (g n)"), sp[:, :], ACT.Copy).then_inc(pt_copied, 1)

            def gelus(t, l, first=False, more=1):
                if not first:
                    eng.wait_ge(ff_ready, G * t)
                for m in range(KH):
                    eng.wait_ge(hid_ready, KH * t + m + 1)
                    if not (first and m < HB):
                        eng.wait_ge(gl_done, KH * t + reuse(m))
                    eng.activation(g32[:, m % HB, :], hid[m % HB][:, :], ACT.Gelu, scale=1.0 / WS,
                                   bias=b1c[:, l, m:m + 1]).then_inc(gelu_done, 1)
                    eng.wait_ge(gelu_done, KH * t + m + 1)
                    eng.activation(gt[:, 0, m, :], g32[:, m % HB, :], ACT.Copy).then_inc(gh_done, 1)
                    if m == PT_AT and more:
                        pt_copy(t + 1)

            exps(0)
            pt_copy(0)
            heads(0)
            exps(1)
            eng.wait_ge(b1_ready, L)
            gelus(0, 0, first=True)
            heads(1)
            exps(2)
            with eng.Fori(1, STEPS - 2) as t:
                gelus(t, layer(t))
                heads(t + 1)
                exps(t + 2)
            gelus(STEPS - 2, L - 1)
            heads(STEPS - 1)
            gelus(STEPS - 1, L - 1, more=0)

        @block.tensor
        def _(eng):
            def spread(s):
                eng.wait_ge(cols_done, 2 * G * (s + 1))
                for g in range(G):
                    ins = eng.transpose(sp[:, g * N:(g + 1) * N], sij[:, G + g:G + g + 1].to_broadcast([128, 128]),
                                        ident[:, :])
                ins.then_inc(spread_ready, 1)

            def turn(s):
                eng.wait_ge(exp_done, s + 1)
                for g in range(G):
                    ins = eng.transpose(sp[:, g * N:(g + 1) * N], v[:, g, :], ident[:, :])
                ins.then_inc(pt_ready, 1)

            def gather(s, slot, first=False):
                eng.wait_ge(pt_copied, s + 1)
                eng.wait_ge(x_ready, s + 1)
                if not first:
                    eng.wait_ge(htl_done, KD * s)
                for g in range(G):
                    eng.matmul(pair(agg, g), pts[:, g, :], xs[:, slot, g, :], start=True, stop=True)\
                       .then_inc(agg_ready, 1)

            def shift(l):
                eng.wait_ge(w_in[0], 16 * (l + 1))
                for m in range(KH):
                    for k in range(KD):
                        ins = eng.matmul(ff[0][:, KH * l + m:KH * l + m + 1], stage[:, H * k + 128 * m:H * k + 128 * (m + 1)],
                                         beta1c[:, l, k:k + 1], start=(k == 0), stop=(k == KD - 1))
                ins.then_inc(shift_ready, 1)

            def heads(s):
                eng.wait_ge(z_ready, s + 1)
                for k in range(KD):
                    for g in range(G):
                        ins = eng.transpose(agg[k][:, g * N:(g + 1) * N], z[:, g, k * 128:(k + 1) * 128], ident[:, :])
                    ins.then_inc(ht_ready, 1)

            def up(t, l, first, more):
                for m in range(KH):
                    if m == 0:
                        eng.wait_ge(htl_done, KD * (t + 1))
                    if not (first and m < HB):
                        eng.wait_ge(gelu_done, KH * t + reuse(m))
                    n = 0
                    for k in range(KD):
                        for w, a in ((w1h, 0), (w1h, 1), (w1l, 0)):
                            ins = eng.matmul(hid[m % HB][:, :], w[:, l, k, m * 128:(m + 1) * 128], ht[:, a, k, :],
                                             start=(n == 0), stop=(n == 3 * KD - 1))
                            n += 1
                    ins.then_inc(hid_ready, 1)
                    if m == PT_AT and more >= 1:
                        turn(t + 1)
                    if m == AGG_AT and more >= 1:
                        gather(t + 1, (t + 1) & (NG - 1))

            def down(t, l, g, first=False):
                if g == 0:
                    eng.wait_ge(b1_ready, L) if first else eng.wait_ge(z2_ready, t)
                for k in range(KH):
                    eng.wait_ge(gh_done, KH * t + k + 1) if g == 0 else None
                    eng.wait_ge(gl_done, KH * t + k + 1) if g == 0 else None
                    for a, w in ((0, w2h), (0, w2l), (1, w2h)):
                        ins = eng.matmul(pair(ff, g), gt[:, a, k, g * N:(g + 1) * N], w[:, l, k, :],
                                         start=(k == 0 and a == 0 and w is w2h), stop=(k == KH - 1 and a == 1))
                ins.then_inc(ff_ready, 1)

            eng.wait_ge(const_ready, 2)
            eng.wait_ge(par_in, 16 * 10)
            for l in range(L):
                shift(l)
            spread(0)
            turn(0)
            gather(0, 0, first=True)
            heads(0)
            spread(1)

            def step(t, l, first=False, more=2):
                up(t, l, first, more)
                for g in range(G):
                    down(t, l, g, first)
                    if g == 1 and more >= 2:
                        spread(t + 2)
                    if g == G - 2 and more >= 1:
                        heads(t + 1)

            eng.wait_ge(w_used, (KD + 1) * L)
            eng.wait_ge(w_split, (KD + 1) * L)
            step(0, 0, first=True)
            with eng.Fori(1, STEPS - 2) as t:
                step(t, layer(t))
            step(STEPS - 2, L - 1, more=1)
            step(STEPS - 1, L - 1, more=0)

        @block.vector
        def _(eng):
            def low_halves(l):
                for k in range(KD):
                    eng.wait_ge(w_used, (KD + 1) * l + k + 1)
                    eng.scalar_tensor_tensor(out=w1l[:, l, k, :], in0=stage[:, H * k:H * (k + 1)],
                                             scalar=g1c[:, l, k:k + 1], in1=w1h[:, l, k, :],
                                             op0=ALU.mult, op1=ALU.subtract).then_inc(w_split, 1)
                eng.wait_ge(w_used, (KD + 1) * (l + 1))
                eng.scalar_tensor_tensor(out=w2l[:, l, :, :].rearrange("p k h -> p (k h)"),
                                         in0=stage[:, KD * H:2 * KD * H], scalar=WS,
                                         in1=w2h[:, l, :, :].rearrange("p k h -> p (k h)"),
                                         op0=ALU.mult, op1=ALU.subtract).then_inc(w_split, 1)

            def shift(l):
                eng.wait_ge(shift_ready, l + 1)
                eng.tensor_tensor(out=b1c[:, l, :], in0=b1c[:, l, :], in1=ff[0][:, KH * l:KH * (l + 1)], op=ALU.add)\
                   .then_inc(b1_ready, 1)

            eng.wait_ge(par_in, 16 * 10)
            eng.tensor_scalar(g1c[:, :, :], g1c[:, :, :], WS, None, ALU.mult).then_inc(g1c_ready, 1)
            eng.wait_ge(g1c_ready, 1)
            low_halves(0)
            eng.wait_ge(const_ready, 2)
            for g in range(NG):
                eng.wait_ge(adj_in[g % 2], 16 * (g // 2 + 1))
                if g:
                    eng.wait_ge(init_chain, g + 1)
                eng.scalar_tensor_tensor(out=edge, in0=adji[:, g % 2, :, :], scalar=0.0,
                                         in1=ident[:, :].unsqueeze(1).to_broadcast([128, G, N]),
                                         op0=ALU.is_gt, op1=ALU.max).then_inc(adj_used, 1)
                eng.wait_ge(adj_used, g + 1)
                eng.tensor_scalar(mask[:, g, :, :], edge, 1.0, FAR, ALU.subtract, ALU.mult).then_inc(init_chain, 1)
            for l in range(1, L):
                low_halves(l)
            eng.wait_ge(init_chain, NG + 1)

            def cols(s, slot, l, graphs=range(G), first=False):
                eng.wait_ge(x_ready, s + 1)
                for g in graphs:
                    for a in range(2):
                        if not first or g:
                            eng.wait_ge(cols_done, 2 * G * s + 2 * g + a - 1)
                        ins = eng.scalar_tensor_tensor(out=junk[:, a, :], in0=xs[:, slot, g, :], scalar=1.0,
                                                       in1=aw[:, l, a * D:(a + 1) * D], op0=ALU.mult, op1=ALU.mult,
                                                       accum_out=sij[:, a * G + g:a * G + g + 1])
                        ins.then_inc(cols_done, 1)

            def scores(s, l):
                eng.wait_ge(cols_done, 2 * G * (s + 1))
                eng.wait_ge(spread_ready, s + 1)
                eng.scalar_tensor_tensor(out=v[:, :, :], in0=sp[:, :].rearrange("p (g n) -> p g n", g=G),
                                         scalar=ab[:, l:l + 1] if isinstance(l, int) else ab[:, bass.ds(l, 1)],
                                         in1=sij[:, 0:G].unsqueeze(2).to_broadcast([128, G, N]),
                                         op0=ALU.add, op1=ALU.add).then_inc(score_chain, 1)

            def scores_end(s, slot):
                eng.wait_ge(score_chain, 3 * s + 1)
                eng.scalar_tensor_tensor(out=v[:, :, :], in0=v[:, :, :], scalar=SLOPE, in1=v[:, :, :],
                                         op0=ALU.mult, op1=ALU.max).then_inc(score_chain, 1)
                eng.wait_ge(score_chain, 3 * s + 2)
                eng.tensor_tensor(out=v[:, :, :], in0=v[:, :, :], in1=mask[:, slot, :, :], op=ALU.add)\
                   .then_inc(score_chain, 1)
                eng.wait_ge(score_chain, 3 * s + 3)
                eng.tensor_reduce(nm[:, :], v[:, :, :], AX.X, ALU.max, negate=True).then_inc(scores_ready, 1)

            def recip(s):
                eng.wait_ge(exp_done, s + 1)
                eng.reciprocal(rinv[:, :], rs[:, :]).then_inc(rinv_ready, 1)

            def moments(zt, st, mv, ve, chain, base, var_ready):
                for g in range(G):
                    eng.wait_ge(chain, base + G + g)
                    eng.bn_stats(st[:, g, :], zt[:, g, :]).then_inc(chain, 1)
                    if g:
                        ins = eng.bn_aggr(mv[:, g - 1, :], st[:, g - 1, :])
                ins.then_inc(chain, 1)
                eng.wait_ge(chain, base + 2 * G + 1)
                eng.tensor_scalar(ve[:, 0:G - 1], mv[:, 0:G - 1, 1], EPS, None, ALU.add)
                eng.bn_aggr(mv[:, G - 1, :], st[:, G - 1, :]).then_inc(chain, 1)
                eng.wait_ge(chain, base + 2 * G + 2)
                eng.tensor_scalar(ve[:, G - 1:G], mv[:, G - 1:G, 1], EPS, None, ALU.add).then_inc(var_ready, 1)

            def gathered(s, slot, graphs=range(G), first=False):
                if not first and 0 in graphs:
                    eng.wait_ge(hb_ready, s)
                    eng.wait_ge(ht_ready, KD * s)
                eng.wait_ge(rinv_ready, s + 1)
                for g in graphs:
                    eng.wait_ge(agg_ready, G * s + g // 2 * 2 + 2)
                    eng.scalar_tensor_tensor(out=z[:, g, :], in0=pair(agg, g), scalar=rinv[:, g:g + 1],
                                             in1=xs[:, slot, g, :], op0=ALU.mult, op1=ALU.add).then_inc(ln1_chain, 1)

            def norm1(s):
                moments(z, st1, mv1, ve1, ln1_chain, (2 * G + 2) * s, var1_ready)

            def norm1_end(s):
                eng.wait_ge(rstd1_ready, s + 1)
                for g in range(G):
                    ins = eng.tensor_scalar(z[:, g, :], z[:, g, :], mv1[:, g, 0:1], rstd1[:, g:g + 1],
                                            ALU.subtract, ALU.mult)
                ins.then_inc(z_ready, 1)

            def head_low(s):
                for k in range(KD):
                    eng.wait_ge(hth_done, KD * s + k + 1)
                    eng.tensor_tensor(out=ht[:, 1, k, :], in0=agg[k][:, :], in1=ht[:, 0, k, :], op=ALU.subtract)\
                       .then_inc(htl_done, 1)

            def gelu_low(t, m):
                eng.wait_ge(gh_done, KH * t + m + 1)
                eng.tensor_tensor(out=gt[:, 1, m, :], in0=g32[:, m % HB, :], in1=gt[:, 0, m, :], op=ALU.subtract)\
                   .then_inc(gl_done, 1)

            def residual2(t, i, first=False):
                if i == 0:
                    eng.wait_ge(hb_ready, t + 1)
                    if not first:
                        eng.wait_ge(x_stored, t)
                eng.wait_ge(ff_ready, G * t + 2 * i + 2)
                eng.scalar_tensor_tensor(out=z2[:, 2 * i:2 * i + 2, :].rearrange("p g d -> p (g d)"),
                                         in0=ff[i][:, :], scalar=1.0 / WS,
                                         in1=hb[:, t & 1, 2 * i:2 * i + 2, :].rearrange("p g d -> p (g d)"),
                                         op0=ALU.mult, op1=ALU.add).then_inc(ln2_chain, 2)

            def norm2(t):
                moments(z2, st2, mv2, ve2, ln2_chain, (2 * G + 2) * t, var2_ready)

            def norm2_end(t):
                eng.wait_ge(rstd2_ready, t + 1)
                for g in range(G):
                    ins = eng.tensor_scalar(z2[:, g, :], z2[:, g, :], mv2[:, g, 0:1], rstd2[:, g:g + 1],
                                            ALU.subtract, ALU.mult)
                ins.then_inc(z2_ready, 1)

            cols(0, 0, 0, first=True)
            scores(0, 0)
            scores_end(0, 0)
            recip(0)
            gathered(0, 0, first=True)
            norm1(0)
            norm1_end(0)
            head_low(0)
            cols(1, 1, 0)
            scores(1, 0)
            scores_end(1, 1)
            for l in range(L):
                shift(l)

            def step(t, first=False, more=2):
                if not first:
                    residual2(t - 1, 1)
                    norm2(t - 1)
                gelu_low(t, 0)
                gelu_low(t, 1)
                if not first:
                    norm2_end(t - 1)
                for m in range(2, KH):
                    if m == KH - 1 and more >= 1:
                        gathered(t + 1, (t + 1) & (NG - 1), (0,))
                    gelu_low(t, m)
                    if m >= KH - 1 - G and m < KH - 1 and more >= 2:
                        cols(t + 2, (t + 2) & (NG - 1), layer(t + 2), [m - (KH - 1 - G)])
                    if m == KH - 3 and more >= 1:
                        recip(t + 1)
                if more >= 1:
                    gathered(t + 1, (t + 1) & (NG - 1), range(1, G))
                    norm1(t + 1)
                if more >= 2:
                    scores(t + 2, layer(t + 2))
                if more >= 1:
                    norm1_end(t + 1)
                if more >= 2:
                    scores_end(t + 2, (t + 2) & (NG - 1))
                if more >= 1:
                    head_low(t + 1)
                residual2(t, 0, first)

            step(0, first=True)
            with eng.Fori(1, STEPS - 2) as t:
                step(t)
            step(STEPS - 2, more=1)
            step(STEPS - 1, more=0)
            residual2(STEPS - 1, 1)
            norm2(STEPS - 1)
            norm2_end(STEPS - 1)


def wait(eng, sem, value):
    if not isinstance(value, int) or value > 0:
        eng.wait_ge(sem, value)


def other_networks(nc, xs, ident, half, bank, x, adj, w1g, a1g, w2g, bias, w3, b3_down, attn3, out):
    ctx = ExitStack()
    with ctx:
        def sb(name, shape, dt=F32):
            return ctx.enter_context(nc.sbuf_tensor(name, shape, dt))

        sems = {}

        def sem(name):
            sems[name] = ctx.enter_context(nc.semaphore(name))
            return sems[name]

        wf = sb("wf", [128, KD, D])
        wa = sb("wa", [128, KD, 2])
        wm = sb("wm", [128, KD, D])
        biasm = sb("biasm", [128, D])
        wb = sb("wb", [128, KD, D])
        wat = sb("wat", [128, KD, D])
        bc = sb("bc", [128, KD])
        identb = sb("identb", [128, 128], BF16)
        pick = sb("pick", [128, 4, 32], BF16)
        xin = sb("xin", [128, 2, G, D])
        adji = sb("adji2", [128, 2, G, N], I32)
        lab = sb("lab", [128, 4, G, N], BF16)
        r1 = sb("r1", [128, G, D])
        u1 = [sb(f"u1_{i}", [128, G, D]) for i in range(2)]
        u1t = sb("u1t", [128, KD, T])
        wh = sb("wh", [128, G, D])
        ec = sb("ec", [128, 2 * G])
        mkf = sb("mkf", [128, G, N], BF16)
        vf = sb("vf", [128, G, N])
        left = sb("left", [128, G, N])
        top = sb("top", [128, G, 2, 8])
        pause = sb("pause", [128, 1])
        nmf = sb("nmf", [128, G])
        rsf = sb("rsf", [128, G])
        rif = sb("rif", [128, G])
        ptf = sb("ptf", [128, G, N])
        negf = sb("negf", [128, G, D])
        posf = sb("posf", [128, G, D])
        r2 = sb("r2", [128, G, D])
        u2 = sb("u2", [128, G, D])
        u2t = sb("u2t", [128, KD, T])
        labt = sb("labt", [128, T], BF16)
        hot = sb("hot", [128, 16, T], BF16)
        cnt = sb("cnt", [128, T])
        r3 = sb("r3", [128, G, D])
        u3 = [sb(f"u3_{i}", [128, G, D]) for i in range(2)]
        u3t = sb("u3t", [128, KD, T])
        hh = sb("hh", [128, G, D])
        hht = sb("hht", [128, KD, T])
        hat = sb("hat", [128, KD, T])
        mkb = sb("mkb", [128, G, N], BF16)
        vb = sb("vb", [128, G, N])
        nmb = sb("nmb", [128, G])
        rsb = sb("rsb", [128, G])
        rib = sb("rib", [128, G])
        rib_less = sb("rib_less", [128, G])
        ptb = sb("ptb", [128, G, N])
        negb = sb("negb", [128, G, D])
        posb = sb("posb", [128, G, D])
        y = sb("y", [128, G, D])
        wm2 = y[:, :, :].rearrange("p (w k) o -> p w k o", k=KD)
        ab2 = negb[:, 0:2, :]

        class Norm:

            def __init__(self, name):
                self.st = sb(name + "_st", [128, G, 6])
                self.mv = sb(name + "_mv", [128, G, 2])
                self.ve = sb(name + "_ve", [128, G])
                self.rstd = sb(name + "_rstd", [128, G])
                self.drop = sb(name + "_drop", [128, G])
                self.shift = sb(name + "_shift", [128, G])
                self.chain = sem(name + "_chain")
                self.var_ready = sem(name + "_var_ready")
                self.rstd_ready = sem(name + "_rstd_ready")
                self.done = sem(name + "_done")
                self.drop_ready = sem(name + "_drop_ready")
                self.shift_ready = sem(name + "_shift_ready")

        n1, n2, n3, n4 = Norm("n1"), Norm("n2"), Norm("n3"), Norm("n4")

        fp, fs = bank[0:2], bank[2]
        mp = bank[3:5]
        bp, bs = bank[5:7], bank[7]

        def pair(banks, g):
            return banks[g // 2][:, (g % 2) * D:(g % 2 + 1) * D]

        def flat(t):
            return t[:, :, :].rearrange("p a b -> p (a b)")

        def half_of(t, i):
            return t[:, 2 * i:2 * i + 2, :].rearrange("p g d -> p (g d)")

        par_in = sem("par2_in")
        const_ready = sem("const2_ready")
        init_chain = sem("init2_chain")
        pick_chain = sem("pick_chain")
        wa_ready = sem("wa_ready")
        x_in = [sem(f"x2_in{i}") for i in range(2)]
        adj_in = [sem(f"adj2_in{i}") for i in range(2)]
        r1_ready = sem("r1_ready")
        lab_ready = sem("lab_ready")
        u1_turned, u1t_done = sem("u1_turned"), sem("u1t_done")
        wh_ready, wh_done = sem("wh_ready"), sem("wh_done")
        ec_ready, ec_done = sem("ec_ready"), sem("ec_done")
        fspread = sem("fspread")
        fchain = sem("fchain")
        fscores = sem("fscores")
        fexp = sem("fexp")
        fri = sem("fri")
        ftop_chain = sem("ftop_chain")
        ftop = sem("ftop")
        fturn, fturn_done = sem("fturn"), sem("fturn_done")
        fagg = sem("fagg")
        fneg, fpos, fexpn = sem("fneg"), sem("fpos"), sem("fexpn")
        fsum = sem("fsum")
        u2_raw = sem("u2_raw")
        lab_turned, labt_done = sem("lab_turned"), sem("labt_done")
        hot_ready = sem("hot_ready")
        cnt_ready, cnt_done = sem("cnt_ready"), sem("cnt_done")
        u2_turned, u2t_done = sem("u2_turned"), sem("u2t_done")
        mout = sem("mout")
        r3_ready = sem("r3_ready")
        u3_turned, u3t_done = sem("u3_turned"), sem("u3t_done")
        hht_ready, hht_done = sem("hht_ready"), sem("hht_done")
        hat_ready, hat_done = sem("hat_ready"), sem("hat_done")
        hh_ready, hh_done = sem("hh_ready"), sem("hh_done")
        bsc = sem("bsc")
        bchain = sem("bchain")
        bscores = sem("bscores")
        bexp = sem("bexp")
        bri = sem("bri")
        bturn, bturn_done = sem("bturn"), sem("bturn_done")
        bagg = sem("bagg")
        bneg, bpos, bexpn = sem("bneg"), sem("bpos"), sem("bexpn")
        bsum = sem("bsum")
        y_raw = sem("y_raw")
        out_done = sem("out_done")

        block = ctx.enter_context(nc.Block())

        def steps(eng, step):
            for i in range(-3, 3):
                step(i, i % 2)
            with eng.Fori(0, (NG - 6) // 2) as h:
                step(2 * h + 3, 1)
                step(2 * h + 4, 0)
            for i in range(NG - 3, NG + 1):
                step(i, i % 2)

        def there(s):
            return not isinstance(s, int) or 0 <= s < NG

        @block.sync
        def _(eng):
            for dst, src in (
                (wf[:, :, :], w1g.rearrange("(k p) o -> p k o", p=128)),
                (ab2[:, :, :], a1g.partition_broadcast(128)),
                (y[:, :, :], w2g.rearrange("(w k p) o -> p (w k) o", p=128, k=KD)),
                (wb[:, :, :], w3.rearrange("(k p) o -> p k o", p=128)),
                (wat[:, :, :], attn3.rearrange("(k p) o -> p k o", p=128)),
                (bc[:, :], b3_down),
            ):
                eng.dma_start(dst, src).then_inc(par_in, 16)
            eng.wait_ge(const_ready, 1)
            for c in range(4):
                eng.dma_start(biasm[32 * c:32 * c + 4, :], bias[c]).then_inc(par_in, 16)

            def load(s, b):
                eng.dma_start(adji[:, b, :, :], adj[s].rearrange("g i j -> i g j")).then_inc(adj_in[b], 16)
                eng.dma_start(xin[:, b, :, :], x[s].rearrange("g n d -> n g d")).then_inc(x_in[b], 16)

            def store(s):
                eng.wait_ge(n4.done, s + 1)
                eng.dma_start(out[s].rearrange("g n d -> n g d"), y[:, :, :]).then_inc(out_done, 16)

            load(0, 0)
            load(1, 1)
            for s in range(2, 6):
                eng.wait_ge(lab_ready, s - 1)
                eng.wait_ge(r1_ready, s - 1)
                load(s, s % 2)
            with eng.Fori(0, (NG - 6) // 2) as h:
                for b in range(2):
                    eng.wait_ge(lab_ready, 2 * h + 5 + b)
                    eng.wait_ge(r1_ready, 2 * h + 5 + b)
                    load(2 * h + 6 + b, b)
                    store(2 * h + b)
            for s in range(NG - 6, NG):
                store(s)
            eng.wait_ge(out_done, 16 * NG)

        @block.gpsimd
        def _(eng):
            eng.memset(biasm[:, :], 0.0).then_inc(const_ready, 1)
            eng.memset(pick[:, :, :], 0.0).then_inc(pick_chain, 1)
            eng.tensor_copy(identb[:, :], ident[:, :]).then_inc(const_ready, 1)
            eng.wait_ge(pick_chain, 1)
            eng.affine_select(out=pick[:, :, :], in_=pick[:, :, :], compare_op=ALU.not_equal, fill=1.0,
                              base=0, pattern=[[1, 4], [-1, 32]], channel_multiplier=0).then_inc(const_ready, 1)

            def root(n, s, shift=False):
                if there(s):
                    eng.wait_ge(n.var_ready, s + 1)
                    eng.tensor_tensor(out=n.rstd[:, :], in0=n.ve[:, :], in1=half[:, :], op=ALU.pow)\
                       .then_inc(n.rstd_ready, 1)
                    if shift:
                        eng.tensor_scalar(n.drop[:, :], n.mv[:, :, 0], -1.0, None, ALU.mult)\
                           .then_inc(n.drop_ready, 1)
                        eng.wait_ge(n.rstd_ready, s + 1)
                        eng.wait_ge(n.drop_ready, s + 1)
                        eng.tensor_tensor(out=n.shift[:, :], in0=n.drop[:, :], in1=n.rstd[:, :], op=ALU.mult)\
                           .then_inc(n.shift_ready, 1)

            def enter(s, b):
                if there(s):
                    eng.wait_ge(adj_in[b], 16 * (s // 2 + 1) if isinstance(s, int) else ((s >> 1) + 1) * 16)
                    wait(eng, n1.done, s)
                    wait(eng, bscores, s - 3)
                    eng.tensor_copy(lab[:, s & 3, :, :], adji[:, b, :, :]).then_inc(lab_ready, 1)
                    eng.wait_ge(x_in[b], 16 * (s // 2 + 1) if isinstance(s, int) else ((s >> 1) + 1) * 16)
                    eng.tensor_tensor(out=r1[:, :, :], in0=xin[:, b, :, :], in1=xs[:, s, :, :], op=ALU.add)\
                       .then_inc(r1_ready, 1)

            def add_pos(s, total, total_ready, pos, pos_ready, raw):
                if there(s):
                    eng.wait_ge(total_ready, s + 1)
                    eng.wait_ge(pos_ready, s + 1)
                    eng.tensor_tensor(out=total[:, :, :], in0=total[:, :, :], in1=pos[:, :, :], op=ALU.add)\
                       .then_inc(raw, 1)

            def step(i, own):
                root(n3, i)
                enter(i + 3, 1 - own)
                add_pos(i - 1, y, bsum, posb, bpos, y_raw)
                root(n2, i + 1)
                root(n1, i + 3, shift=True)
                root(n4, i - 1, shift=True)
                add_pos(i + 2, r2, fsum, posf, fpos, u2_raw)

            steps(eng, step)

        @block.scalar
        def _(eng):
            eng.wait_ge(par_in, 16 * 10)

            def banks_out(s, banks, ready, dst, done, bias_col=None):
                if there(s):
                    for k in range(2):
                        eng.wait_ge(ready, 2 * s + k + 1)
                        if bias_col is None:
                            eng.activation(dst(k), banks[k][:, :], ACT.Copy).then_inc(done, 1)
                        else:
                            eng.activation(dst(k), banks[k][:, :], ACT.Identity, bias=bias_col[:, k:k + 1])\
                               .then_inc(done, 1)

            def one_out(s, src, ready, dst, done):
                if there(s):
                    eng.wait_ge(ready, s + 1)
                    eng.activation(dst, src, ACT.Copy).then_inc(done, 1)

            def exps(s, vt, nm, rs, scores_ready, done):
                if there(s):
                    eng.wait_ge(scores_ready, s + 1)
                    for g in range(G):
                        ins = eng.activation(vt[:, g, :], vt[:, g, :], ACT.Exp, bias=nm[:, g:g + 1],
                                             accum_out=rs[:, g:g + 1])
                    ins.then_inc(done, 1)

            def elu(s, banks, agg_ready, ri, ri_ready, pos, pos_ready, neg, neg_ready, expn, raw):
                if there(s):
                    eng.wait_ge(ri_ready, s + 1)
                    wait(eng, raw, s)
                    for g in range(G):
                        eng.wait_ge(agg_ready, G * s + g // 2 * 2 + 2)
                        eng.wait_ge(neg_ready, 2 * s + g // 2 + 1)
                        ins = eng.activation(pos[:, g, :], pair(banks, g), ACT.Relu, scale=ri[:, g:g + 1])
                    ins.then_inc(pos_ready, 1)
                    eng.activation(flat(neg), flat(neg), ACT.Exp).then_inc(expn, 1)

            def elu_alone(s):
                if there(s):
                    eng.wait_ge(bri, 2 * s + 2)
                    wait(eng, y_raw, s)
                    wait(eng, bsum, s)
                    for g in range(G):
                        eng.wait_ge(bagg, G * s + g // 2 * 2 + 2)
                        eng.activation(negb[:, g, :], pair(bp, g), ACT.Relu, scale=rib_less[:, g:g + 1])\
                           .then_inc(bneg, 1)
                        ins = eng.activation(posb[:, g, :], pair(bp, g), ACT.Relu, scale=rib[:, g:g + 1])
                    ins.then_inc(bpos, 1)
                    eng.wait_ge(bneg, G * s + G)
                    eng.activation(flat(negb), flat(negb), ACT.Exp, scale=-1.0).then_inc(bexpn, 1)

            def normed(s, n, src, dst, readers, graphs=range(G)):
                if there(s):
                    eng.wait_ge(n.shift_ready, s + 1)
                    for reader, count in readers:
                        wait(eng, reader, count)
                    for g in graphs:
                        ins = eng.activation(dst[:, g, :], src[:, g, :], ACT.Identity, scale=n.rstd[:, g:g + 1],
                                             bias=n.shift[:, g:g + 1])
                    if graphs[-1] == G - 1:
                        ins.then_inc(n.done, 1)

            def step(i, own):
                banks_out(i + 2, fp, u1_turned, lambda k: u1t[:, k, :], u1t_done)
                normed(i - 2, n4, y, y, [], (2, 3))
                one_out(i + 1, mp[0][:, :].bitcast(BF16)[:, 0:T], lab_turned, labt[:, :], labt_done)
                elu_alone(i - 1)
                banks_out(i + 2, fp, wh_ready, lambda k: half_of(wh, k), wh_done)
                banks_out(i, bp, u3_turned, lambda k: u3t[:, k, :], u3t_done)
                one_out(i + 2, fs[:, 0:2 * G], ec_ready, ec[:, :], ec_done)
                banks_out(i, bp, hht_ready, lambda k: hht[:, k, :], hht_done, bc)
                one_out(i + 1, mp[1][:, :], cnt_ready, cnt[:, :], cnt_done)
                exps(i + 2, vf, nmf, rsf, fscores, fexp)
                banks_out(i, bp, hat_ready, lambda k: hat[:, k, :], hat_done)
                banks_out(i + 1, mp, u2_turned, lambda k: u2t[:, k, :], u2t_done)
                one_out(i + 2, fs[:, :], fturn, flat(ptf), fturn_done)
                banks_out(i, bp, hh_ready, lambda k: half_of(hh, k), hh_done)
                exps(i, vb, nmb, rsb, bscores, bexp)
                elu(i + 2, fp, fagg, rif, fri, posf, fpos, negf, fneg, fexpn, u2_raw)
                one_out(i, bs[:, :], bturn, flat(ptb), bturn_done)
                normed(i + 3, n1, r1, u1[1 - own], [(fsum, i + 2), (u1_turned, 2 * (i + 2))])
                normed(i - 1, n4, y, y, [], (0, 1))

            steps(eng, step)
            normed(NG - 1, n4, y, y, [], (2, 3))

        @block.tensor
        def _(eng):
            eng.wait_ge(par_in, 16 * 10)
            eng.wait_ge(const_ready, 3)
            eng.wait_ge(wa_ready, 5)

            def turn_features(s, src, src_ready, banks, turned, bank_free, free_count):
                if there(s):
                    eng.wait_ge(src_ready, s + 1)
                    wait(eng, bank_free, free_count)
                    for k in range(KD):
                        for g in range(G):
                            ins = eng.transpose(banks[k][:, g * N:(g + 1) * N], src[:, g, k * 128:(k + 1) * 128],
                                                ident[:, :])
                        ins.then_inc(turned, 1)

            def turn_probs(s, src, src_ready, bank_, turned):
                if there(s):
                    eng.wait_ge(src_ready, s + 1)
                    for g in range(G):
                        ins = eng.transpose(bank_[:, g * N:(g + 1) * N], src[:, g, :], ident[:, :])
                    ins.then_inc(turned, 1)

            def turn_labels(s):
                if there(s):
                    eng.wait_ge(lab_ready, s + 1)
                    wait(eng, r3_ready, 2 * s)
                    for g in range(G):
                        ins = eng.transpose(mp[0][:, :].bitcast(BF16)[:, g * N:(g + 1) * N],
                                            lab[:, s & 3, g, :], identb[:, :])
                    ins.then_inc(lab_turned, 1)

            def project(s):
                if there(s):
                    eng.wait_ge(u1t_done, 2 * s + 2)
                    for g in range(G):
                        for k in range(KD):
                            ins = eng.matmul(pair(fp, g), u1t[:, k, g * N:(g + 1) * N], wf[:, k, :],
                                             start=(k == 0), stop=(k == KD - 1))
                        if g % 2:
                            ins.then_inc(wh_ready, 1)

            def score_columns(s):
                if there(s):
                    wait(eng, fturn_done, s)
                    for g in range(G):
                        for k in range(KD):
                            ins = eng.matmul(fs[:, 2 * g:2 * g + 2], u1t[:, k, g * N:(g + 1) * N], wa[:, k, :],
                                             start=(k == 0), stop=(k == KD - 1))
                    ins.then_inc(ec_ready, 1)

            def spread(s):
                if there(s):
                    eng.wait_ge(ec_done, s + 1)
                    for g in range(G):
                        ins = eng.transpose(fs[:, g * N:(g + 1) * N],
                                            ec[:, 2 * g + 1:2 * g + 2].to_broadcast([128, 128]), ident[:, :])
                    ins.then_inc(fspread, 1)

            def gather(s, pt, pt_done, feats, feats_done, feats_count, banks, ready, graphs=range(G)):
                if there(s):
                    eng.wait_ge(pt_done, s + 1)
                    eng.wait_ge(feats_done, feats_count)
                    for g in graphs:
                        eng.matmul(pair(banks, g), pt[:, g, :], feats[:, g, :], start=True, stop=True)\
                           .then_inc(ready, 1)

            def count(s):
                if there(s):
                    for q in range(4):
                        eng.wait_ge(hot_ready, 4 * s + q + 1)
                        for c in range(4):
                            ins = eng.matmul(mp[1][32 * c:32 * c + 32, :], pick[:, q, :], hot[:, 4 * q + c, :],
                                             start=(q == 0), stop=(q == 3), tile_position=(0, 32 * c))
                    ins.then_inc(cnt_ready, 1)

            def mid(s, a):
                if there(s):
                    eng.wait_ge(u2t_done, 2 * s + 2)
                    eng.wait_ge(cnt_done, s + 1)
                    for g in (2 * a, 2 * a + 1):
                        for k in range(KD):
                            eng.matmul(pair(mp, g), u2t[:, k, g * N:(g + 1) * N], wm[:, k, :],
                                       start=(k == 0), stop=False)
                        ins = eng.matmul(pair(mp, g), cnt[:, g * N:(g + 1) * N], biasm[:, :], start=False, stop=True)
                        if g % 2:
                            ins.then_inc(mout, 1)

            def across(s, o, w, src, src_done, done):
                if there(s):
                    eng.wait_ge(src_done, 2 * s + 2)
                    for k in range(KD):
                        ins = eng.matmul(bp[o][:, :], w[:, k, o * 128:(o + 1) * 128], src[:, k, :],
                                         start=(k == 0), stop=(k == KD - 1))
                    ins.then_inc(done, 1)

            def turn_back(s):
                if there(s):
                    eng.wait_ge(hat_done, 2 * s + 2)
                    for g in range(G):
                        for k in range(KD):
                            ins = eng.transpose(pair(bp, g)[:, k * 128:(k + 1) * 128], hht[:, k, g * N:(g + 1) * N],
                                                ident[:, :])
                        if g % 2:
                            ins.then_inc(hh_ready, 1)

            def back_scores(s):
                if there(s):
                    wait(eng, bturn_done, s)
                    eng.wait_ge(hat_done, 2 * s + 2)
                    for g in range(G):
                        for k in range(KD):
                            ins = eng.matmul(bs[:, g * N:(g + 1) * N], hat[:, k, g * N:(g + 1) * N],
                                             hht[:, k, g * N:(g + 1) * N], start=(k == 0), stop=(k == KD - 1))
                    ins.then_inc(bsc, 1)

            def step(i, own):
                f, m, b = i + 2, i + 1, i
                gather(b - 1, ptb, bturn_done, hh, hh_done, 2 * b, bp, bagg, (0, 1))
                turn_features(f, u1[own], n1.done, fp, u1_turned, fpos, f)
                gather(b - 1, ptb, bturn_done, hh, hh_done, 2 * b, bp, bagg, (2, 3))
                turn_labels(m)
                project(f)
                turn_features(b, u3[own], n3.done, bp, u3_turned, bpos, b)
                score_columns(f)
                across(b, 0, wb, u3t, u3t_done, hht_ready)
                spread(f)
                across(b, 1, wb, u3t, u3t_done, hht_ready)
                count(m)
                across(b, 0, wat, hht, hht_done, hat_ready)
                across(b, 1, wat, hht, hht_done, hat_ready)
                if there(m):
                    eng.wait_ge(labt_done, m + 1)
                    eng.wait_ge(cnt_done, m + 1)
                turn_features(m, u2, n2.done, mp, u2_turned, r3_ready, 2 * m)
                back_scores(b)
                turn_probs(f, vf, ftop, fs, fturn)
                turn_back(b)
                gather(f, ptf, fturn_done, wh, wh_done, 2 * f + 2, fp, fagg)
                mid(m, 0)
                turn_probs(b, vb, bexp, bs, bturn)
                mid(m, 1)

            steps(eng, step)

        @block.vector
        def _(eng):
            eng.wait_ge(par_in, 16 * 10)
            eng.tensor_tensor(out=flat(wm), in0=wm2[:, 0, :, :].rearrange("p k o -> p (k o)"),
                              in1=wm2[:, 1, :, :].rearrange("p k o -> p (k o)"), op=ALU.add).then_inc(wa_ready, 1)
            for k in range(KD):
                for a in range(2):
                    eng.scalar_tensor_tensor(out=negf[:, 2 * k + a, :], in0=wf[:, k, :], scalar=1.0,
                                             in1=ab2[:, a, :], op0=ALU.mult, op1=ALU.mult,
                                             accum_out=wa[:, k, a:a + 1]).then_inc(wa_ready, 1)
            eng.wait_ge(wa_ready, 5)

            def moments(s, n, src, ready):
                if there(s):
                    eng.wait_ge(ready, s + 1)
                    base = (G + 2) * s
                    for g in range(G):
                        if g:
                            eng.wait_ge(n.chain, base + g)
                        eng.bn_stats(n.st[:, g, :], src[:, g, :]).then_inc(n.chain, 1)
                        if g:
                            ins = eng.bn_aggr(n.mv[:, g - 1, :], n.st[:, g - 1, :])
                    ins.then_inc(n.chain, 1)
                    eng.wait_ge(n.chain, base + G + 1)
                    eng.tensor_scalar(n.ve[:, 0:G - 1], n.mv[:, 0:G - 1, 1], EPS, None, ALU.add)
                    eng.bn_aggr(n.mv[:, G - 1, :], n.st[:, G - 1, :]).then_inc(n.chain, 1)
                    eng.wait_ge(n.chain, base + G + 2)
                    eng.tensor_scalar(n.ve[:, G - 1:G], n.mv[:, G - 1:G, 1], EPS, None, ALU.add)\
                       .then_inc(n.var_ready, 1)

            def normed(s, n, src, dst, readers=()):
                if there(s):
                    eng.wait_ge(n.rstd_ready, s + 1)
                    for reader, count in readers:
                        wait(eng, reader, count)
                    for g in range(G):
                        ins = eng.tensor_scalar(dst[:, g, :], src[:, g, :], n.mv[:, g, 0:1], n.rstd[:, g:g + 1],
                                                ALU.subtract, ALU.mult)
                    ins.then_inc(n.done, 1)

            def hots(s, part):
                if there(s):
                    eng.wait_ge(labt_done, s + 1)
                    wait(eng, cnt_ready, s)
                    for l in range(4 * part, 4 * part + 4):
                        ins = eng.tensor_scalar(hot[:, l, :], labt[:, :], float(l), None, ALU.is_equal)
                    ins.then_inc(hot_ready, 1)

            def front_scores(s):
                if there(s):
                    eng.tensor_scalar(mkf[:, :, :], lab[:, s & 3, :, :], 0.0, -3e38, ALU.is_equal, ALU.mult)\
                       .then_inc(fchain, 1)
                    eng.wait_ge(fspread, s + 1)
                    wait(eng, fturn, s)
                    src = ec[:, :].rearrange("p (g c) -> p g c", c=2)[:, :, 0:1].to_broadcast([128, G, N])
                    eng.tensor_tensor(out=vf[:, :, :], in0=fs[:, :].rearrange("p (g n) -> p g n", g=G),
                                      in1=src, op=ALU.add).then_inc(fchain, 1)
                    eng.wait_ge(fchain, 4 * s + 2)
                    eng.scalar_tensor_tensor(out=vf[:, :, :], in0=vf[:, :, :], scalar=SLOPE, in1=vf[:, :, :],
                                             op0=ALU.mult, op1=ALU.max).then_inc(fchain, 1)
                    eng.wait_ge(fchain, 4 * s + 3)
                    eng.scalar_tensor_tensor(out=vf[:, :, :], in0=mkf[:, :, :], scalar=FAR / 3e38, in1=vf[:, :, :],
                                             op0=ALU.mult, op1=ALU.add).then_inc(fchain, 1)
                    eng.wait_ge(fchain, 4 * s + 4)
                    eng.tensor_reduce(nmf[:, :], vf[:, :, :], AX.X, ALU.max, negate=True).then_inc(fscores, 1)

            def largest(s):
                if there(s):
                    eng.wait_ge(fexp, s + 1)
                    eng.reciprocal(rif[:, :], rsf[:, :]).then_inc(fri, 1)
                    for g in range(G):
                        ins = eng.max(top[:, g, 0, :], vf[:, g, :])
                    ins.then_inc(ftop_chain, 1)
                    eng.wait_ge(ftop_chain, 5 * s + 1)
                    eng.memset(pause[:, 0:1], 0.0).then_inc(ftop_chain, 1)
                    for g in range(G):
                        ins = eng.match_replace(left[:, g, :], top[:, g, 0, :], vf[:, g, :], -1.0)
                    ins.then_inc(ftop_chain, 1)
                    eng.wait_ge(ftop_chain, 5 * s + 3)
                    eng.memset(pause[:, 0:1], 0.0).then_inc(ftop_chain, 1)
                    for g in range(G):
                        ins = eng.max(top[:, g, 1, :], left[:, g, :])
                    ins.then_inc(ftop_chain, 1)
                    eng.wait_ge(ftop_chain, 5 * s + 5)
                    for g in range(G):
                        ins = eng.scalar_tensor_tensor(out=vf[:, g, :], in0=vf[:, g, :], scalar=top[:, g, 1, 7:8],
                                                       in1=vf[:, g, :], op0=ALU.is_ge, op1=ALU.mult)
                    ins.then_inc(ftop, 1)

            def negatives(s, banks, agg_ready, ri, ri_ready, neg, neg_ready):
                if there(s):
                    eng.wait_ge(ri_ready, s + 1)
                    for g in range(G):
                        eng.wait_ge(agg_ready, G * s + g // 2 * 2 + 2)
                        ins = eng.tensor_scalar(neg[:, g, :], pair(banks, g), ri[:, g:g + 1], 0.0, ALU.mult, ALU.min)
                        if g % 2:
                            ins.then_inc(neg_ready, 1)

            def less_one(s, neg, expn, base, dst, sum_ready, readers=()):
                if there(s):
                    eng.wait_ge(expn, s + 1)
                    for reader, count in readers:
                        wait(eng, reader, count)
                    eng.scalar_tensor_tensor(out=flat(dst), in0=flat(neg), scalar=-1.0, in1=flat(base),
                                             op0=ALU.add, op1=ALU.add).then_inc(sum_ready, 1)

            def mid_sum(s):
                if there(s):
                    for k in range(2):
                        eng.wait_ge(mout, 2 * s + k + 1)
                        eng.scalar_tensor_tensor(out=half_of(r3, k), in0=half_of(u2, k), scalar=2.0,
                                                 in1=mp[k][:, :], op0=ALU.mult, op1=ALU.add).then_inc(r3_ready, 1)

            def back_softmax(s):
                if there(s):
                    eng.tensor_scalar(mkb[:, :, :], lab[:, s & 3, :, :], 0.0, -3e38, ALU.is_equal, ALU.mult)\
                       .then_inc(bchain, 1)
                    eng.wait_ge(bchain, 2 * s + 1)
                    wait(eng, bturn, s)
                    eng.wait_ge(bsc, s + 1)
                    eng.tensor_tensor(out=vb[:, :, :], in0=mkb[:, :, :],
                                      in1=bs[:, :].rearrange("p (g n) -> p g n", g=G), op=ALU.add).then_inc(bchain, 1)
                    eng.wait_ge(bchain, 2 * s + 2)
                    eng.tensor_reduce(nmb[:, :], vb[:, :, :], AX.X, ALU.max, negate=True).then_inc(bscores, 1)

            def back_recip(s):
                if there(s):
                    eng.wait_ge(bexp, s + 1)
                    eng.reciprocal(rib[:, :], rsb[:, :]).then_inc(bri, 1)
                    eng.wait_ge(bri, 2 * s + 1)
                    eng.tensor_scalar(rib_less[:, :], rib[:, :], -1.0, None, ALU.mult).then_inc(bri, 1)

            def step(i, own):
                f, m, b = i + 2, i + 1, i
                if there(b):
                    eng.wait_ge(r3_ready, 2 * b + 2)
                moments(b, n3, r3, n2.done)
                hots(m, 0)
                normed(b, n3, r3, u3[own], [(bsum, b - 1), (u3_turned, 2 * b - 2)])
                hots(m, 1)
                hots(m, 2)
                less_one(b - 1, negb, bexpn, u3[1 - own], y, bsum, [(out_done, 16 * (b - 1))])
                hots(m, 3)
                moments(m, n2, r2, u2_raw)
                front_scores(f)
                normed(m, n2, r2, u2, [(r3_ready, 2 * m), (u2_turned, 2 * m)])
                largest(f)
                back_softmax(b)
                moments(f + 1, n1, r1, r1_ready)
                negatives(f, fp, fagg, rif, fri, negf, fneg)
                back_recip(b)
                moments(b - 1, n4, y, y_raw)
                less_one(f, negf, fexpn, u1[own], r2, fsum, [(n2.done, f)])
                mid_sum(m)

            steps(eng, step)


def layer(s):
    return s // NG if isinstance(s, int) else (s >> (NG.bit_length() - 1)).with_bounds(min_val=0, max_val=L - 1)


def reuse(m):
    held = [i for i in range(KH) if i % HB == m % HB]
    return m - HB + 1 if m >= HB else held[-1] - KH + 1


def build(nc, x, adj, first, others, out):
    with (
        nc.sbuf_tensor("xs", [128, NG, G, D], F32) as xs,
        nc.sbuf_tensor("ident", [128, 128], F32) as ident,
        nc.sbuf_tensor("half", [128, G], F32) as half,
        ExitStack() as ctx,
    ):
        bank = [ctx.enter_context(nc.psum_tensor(f"bank{i}", [128, T], F32)) for i in range(8)]
        first_network(nc, xs, ident, half, bank, x, adj, *first)
        other_networks(nc, xs, ident, half, bank, x, adj, *others, out)


def kernel(**inputs):
    import numpy as np
    import concourse.bacc as bacc
    from concourse.bass_utils import run_bass_kernel_spmd as run

    nc = bacc.Bacc("TRN2", target_bir_lowering=False, num_devices=1)
    arrays = {}

    def give(name, shape=None, order=None, as_name=None):
        a = np.asarray(inputs[name])
        if shape:
            a = a.reshape(shape)
        if order:
            a = a.transpose(order)
        name = "in_" + (as_name or name)
        arrays[name] = np.ascontiguousarray(a)
        return nc.dram_tensor(name, a.shape, mybir.dt.from_np(a.dtype), kind="ExternalInput").ap()

    def down(name):
        return give(name, (L, -1, 128), (2, 0, 1), name + "_down")

    x = give("x", (NG, G, N, D))
    adj = give("adj", (NG, G, N, N))
    first = [give("L0_gnn_attn_w"), give("L0_gnn_attn_b"), give("L0_gnn_W1"), down("L0_gnn_b1"), give("L0_gnn_W2"),
             give("L0_gnn_b2"), give("L0_gnn_g1"), give("L0_gnn_beta1"), give("L0_gnn_g2"), give("L0_gnn_beta2"),
             down("L0_gnn_g1"), down("L0_gnn_beta1")]
    others = [give("L1_gnn_W"), give("L1_gnn_a", (2, D)),
              give("L2_gnn_weights", (2, D, D), (0, 2, 1)).rearrange("w i o -> (w i) o"),
              give("L2_gnn_bias", (4, 4, D), (1, 0, 2)),
              give("L3_gnn_W", None, (1, 0)), give("L3_gnn_b", (KD, 128), (1, 0), "b3_down"),
              give("L3_gnn_attn")]
    out = nc.dram_tensor("out", (NG, G, N, D), F32, kind="ExternalOutput").ap()
    build(nc, x, adj, first, others, out)
    r = run(nc, [arrays], core_ids=[0])
    return r.results[0]["out"].reshape(B, N, D)
```

```python
import concourse.bass as bass
from concourse import mybir
from contextlib import ExitStack

F32, F16, BF16, I32 = mybir.dt.float32, mybir.dt.float16, mybir.dt.bfloat16, mybir.dt.int32
ALU, ACT, AX = mybir.AluOpType, mybir.ActivationFunctionType, mybir.AxisListType

B, N, D = 64, 128, 256
G = 4
NG = B // G
T = G * N
L = 3
KD = D // 128
H = 4 * D
KH = H // 128
STEPS = L * NG
EPS = 1e-5
SLOPE = 0.2
FAR = 9e15
WS = 64.0
HB = 3
PT_AT = 2
NG_FIRST = 4
PIECES = 4 * (L - 1)
AGG_AT = 6


def first_network(nc, xs, xin, adji2, x2_in, adj2_in, ident, half, bank, x, adj, attn_w, attn_b, w1, b1_down, w2, b2, g1, beta1, g2, beta2, g1_down, beta1_down):
    ctx = ExitStack()
    with ctx:
        def sb(name, shape, dt=F32):
            return ctx.enter_context(nc.sbuf_tensor(name, shape, dt))

        def sem(name):
            return ctx.enter_context(nc.semaphore(name))

        mask = sb("mask", [128, NG, G, N], BF16)
        w1h = sb("w1h", [128, L, KD, H], F16)
        w1l = sb("w1l", [128, L, KD, H], F16)
        w2h = sb("w2h", [128, L, KH, D], F16)
        w2l = sb("w2l", [128, L, KH, D], F16)
        aw = sb("aw", [128, L, 2 * D])
        ab = sb("ab", [128, L])
        g1b = sb("g1b", [128, L, D])
        betab = sb("betab", [128, L, D])
        g2b = sb("g2b", [128, L, D])
        beta2b = sb("beta2b", [128, L, D])
        b1c = sb("b1c", [128, L, KH])
        g1c = sb("g1c", [128, L, KD])
        beta1c = sb("beta1c", [128, L, KD])
        gt = sb("gt", [128, 2, KH, T], F16)
        stage = gt[:, :, :, :].rearrange("p a k t -> p (a k t)").bitcast(F32)
        ht = sb("ht", [128, 2, KD, T], F16)
        g32 = sb("g32", [128, HB, T])
        z = sb("z", [128, G, D])
        z2 = sb("z2", [128, G, D])
        hb = sb("hb", [128, 2, G, D])
        v = sb("v", [128, G, N])
        pts = sb("pts", [128, G, N])
        junk = sb("junk", [128, 2, D])
        junk_b2 = g32[:, 0:L, 0:D]
        adji = [t[:, :, :].rearrange("p g d -> p (g d)").rearrange("p (b g n) -> p b g n", b=2, g=G).bitcast(I32)
                for t in (z, z2)]
        edge = ht[:, 0, :, :].rearrange("p k t -> p (k t)").bitcast(F32).rearrange("p (g n) -> p g n", g=G)
        last_w1 = hb[:, :, :, :].rearrange("p b g d -> p (b g d)")
        late = xin[:, :, :, :].rearrange("p b g d -> p b (g d)")
        late_adj = adji2[:, 0, :, :]
        late_edge = adji2[:, 1, 0:2, :].rearrange("p g n -> p (g n)").bitcast(BF16).rearrange("p (g n) -> p g n", g=G)
        off_diag = adji2[:, 1, 2, 0:N // 2].bitcast(BF16)
        one = sb("one", [128, 1])
        sij = sb("sij", [128, 2 * G])
        nm = sb("nm", [128, G])
        rs = sb("rs", [128, G])
        rinv = sb("rinv", [128, G])
        st1 = sb("st1", [128, G, 6])
        mv1 = sb("mv1", [128, G, 2])
        ve1 = sb("ve1", [128, G])
        rstd1 = sb("rstd1", [128, G])
        st2 = sb("st2", [128, G, 6])
        mv2 = sb("mv2", [128, G, 2])
        ve2 = sb("ve2", [128, G])
        rstd2 = sb("rstd2", [128, G])

        hid = bank[0:HB]
        ff = bank[3:5]
        agg = bank[5:7]
        sp = bank[7]

        def pair(banks, g):
            return banks[g // 2][:, (g % 2) * D:(g % 2 + 1) * D]

        cols_in = sem("cols_in")
        cut_in = sem("cut_in")
        gain_in = sem("gain_in")
        late_in = [sem(f"late_in{i}") for i in range(2)]
        last_in = sem("last_in")
        late_scaled = sem("late_scaled")
        late_high = sem("late_high")
        late_low = sem("late_low")
        late_adj_in = sem("late_adj_in")
        late_edge_ready = sem("late_edge_ready")
        late_mask_done = sem("late_mask_done")
        one_ready = sem("one_ready")
        w_in = [sem(f"w_in{i}") for i in range(2)]
        x_in = [sem(f"x_in{i}") for i in range(2)]
        adj_in = [sem(f"adj_in{i}") for i in range(2)]
        mask_chain = sem("mask_chain")
        w_used = sem("w_used")
        shift_ready = sem("shift_ready")
        b1_ready = sem("b1_ready")
        g1c_ready = sem("g1c_ready")
        w_split = sem("w_split")
        const_ready = sem("const_ready")
        init_chain = sem("init_chain")
        x_ready = sem("x_ready")
        cols_done = sem("cols_done")
        spread_ready = sem("spread_ready")
        scores_ready = sem("scores_ready")
        score_chain = sem("score_chain")
        exp_done = sem("exp_done")
        rinv_ready = sem("rinv_ready")
        pt_ready = sem("pt_ready")
        pt_copied = sem("pt_copied")
        agg_ready = sem("agg_ready")
        ln1_chain = sem("ln1_chain")
        var1_ready = sem("var1_ready")
        rstd1_ready = sem("rstd1_ready")
        z_ready = sem("z_ready")
        ht_ready = sem("ht_ready")
        hth_done = sem("hth_done")
        htl_done = sem("htl_done")
        hb_chain = sem("hb_chain")
        hb_ready = sem("hb_ready")
        hid_ready = sem("hid_ready")
        gelu_done = sem("gelu_done")
        gh_done = sem("gh_done")
        gl_done = sem("gl_done")
        ff_ready = sem("ff_ready")
        ln2_chain = sem("ln2_chain")
        var2_ready = sem("var2_ready")
        rstd2_ready = sem("rstd2_ready")
        z2_ready = sem("z2_ready")
        x_chain = sem("x_chain")
        x_stored = sem("x_stored")

        block = ctx.enter_context(nc.Block())

        def piece_place(p):
            return p // 2 % (L - 1) + 1, p >= 2 * (L - 1), p % 2

        def piece_of(p):
            l, second, half_ = piece_place(p)
            if not second:
                return w1[l, 128 * half_:128 * (half_ + 1), :]
            return w2[l, 512 * half_:512 * (half_ + 1), :].rearrange("(k p) d -> p k d", p=128)

        def halves_of(p):
            l, second, half_ = piece_place(p)
            if not second:
                return w1h[:, l, half_, :], w1l[:, l, half_, :], g1c[:, l, half_:half_ + 1]
            return tuple(w[:, l, half_ * (KH // 2):(half_ + 1) * (KH // 2), :].rearrange("p k d -> p (k d)")
                         for w in (w2h, w2l)) + (WS,)

        @block.sync
        def _(eng):
            def load_x(g, b):
                eng.dma_start(xs[:, g, :, :], x[g].rearrange("g n d -> n g d")).then_inc(x_in[b], 16)

            def load_adj(b):
                for i in range(2):
                    eng.dma_start(adji[b][:, i, :, :], adj[2 * b + i].rearrange("g i j -> i g j"))\
                       .then_inc(adj_in[b], 16)

            def load_late_adj(g):
                eng.dma_start(late_adj, adj[g].rearrange("g i j -> i g j")).then_inc(late_adj_in, 16)

            load_x(0, 0)
            load_adj(0)
            eng.dma_start(stage[:, 0:2048].rearrange("p (k h) -> p k h", k=KD),
                          w1[0].rearrange("(k p) h -> p k h", p=128)).then_inc(w_in[0], 16)
            eng.dma_start(stage[:, 2048:4096].rearrange("p (k d) -> p k d", k=KH),
                          w2[0].rearrange("(k p) d -> p k d", p=128)).then_inc(w_in[1], 16)
            load_x(1, 1)
            load_adj(1)
            for k in range(KD):
                eng.dma_start(late[:, k, :], w1[1, 128 * k:128 * (k + 1), :]).then_inc(late_in[k], 16)
            eng.dma_start(last_w1.rearrange("p (k h) -> p k h", k=KD),
                          w1[2].rearrange("(k p) h -> p k h", p=128)).then_inc(last_in, 16)
            load_late_adj(NG_FIRST)
            for g in range(NG):
                eng.wait_ge(x_in[g % 2], 16 * (g // 2 + 1))
                eng.sem_inc(x_ready, 1)
                if g + 2 < NG:
                    load_x(g + 2, g % 2)
            for g in range(NG_FIRST + 1, NG):
                eng.wait_ge(late_edge_ready, 2 * (g - NG_FIRST) - 1)
                load_late_adj(g)
                piece = g - NG_FIRST + 1
                if piece < PIECES:
                    eng.wait_ge(late_low, piece - 1)
                    if piece == 2:
                        eng.wait_ge(shift_ready, 2)
                    eng.dma_start(late[:, piece % 2, :] if piece < 2 * KD else
                                  late[:, piece % 2, :].rearrange("p (k d) -> p k d", d=D),
                                  piece_of(piece)).then_inc(late_in[piece % 2], 16)
            with eng.Fori(NG, STEPS) as s:
                eng.wait_ge(x_stored, s - (NG - 1))
                eng.sem_inc(x_ready, 1)
            eng.wait_ge(late_low, PIECES)
            eng.wait_ge(late_mask_done, NG - NG_FIRST)
            for i in range(2):
                eng.dma_start(adji2[:, i, :, :], adj[i].rearrange("g i j -> i g j")).then_inc(adj2_in[i], 16)
                eng.dma_start(xin[:, i, :, :], x[i].rearrange("g n d -> n g d")).then_inc(x2_in[i], 16)

        @block.gpsimd
        def _(eng):
            eng.memset(ident[:, :], 0.0).then_inc(init_chain, 1)
            eng.memset(half[:, :], -0.5).then_inc(const_ready, 1)
            eng.wait_ge(init_chain, 1)
            eng.affine_select(out=ident[:, :], in_=ident[:, :], compare_op=ALU.not_equal, fill=1.0,
                              base=0, pattern=[[-1, 128]], channel_multiplier=1).then_inc(const_ready, 1)
            eng.wait_ge(const_ready, 2)
            eng.memset(one[:, :], 1.0).then_inc(one_ready, 1)
            eng.tensor_scalar(off_diag[:, :], ident[:, :], 1.0, FAR, ALU.subtract, ALU.mult).then_inc(init_chain, 1)
            for tile, src in ((g1b, g1), (betab, beta1), (junk_b2, b2), (g2b, g2), (beta2b, beta2)):
                eng.dma_start(tile[:, :, :] if tile is not junk_b2 else tile, src.partition_broadcast(128))\
                   .then_inc(gain_in, 16)
            eng.wait_ge(gain_in, 16 * 5)
            eng.tensor_tensor(out=betab[:, :, :], in0=betab[:, :, :], in1=junk_b2, op=ALU.add)\
               .then_inc(hb_chain, 1)

            def wide(t, l):
                return t[:, l, :].unsqueeze(1).to_broadcast([128, G, D])

            def root(var_ready, rstd_ready, ve, rstd, s):
                eng.wait_ge(var_ready, s + 1)
                eng.tensor_tensor(out=rstd[:, :], in0=ve[:, :], in1=half[:, :], op=ALU.pow).then_inc(rstd_ready, 1)

            def gain1(s, l):
                eng.wait_ge(z_ready, s + 1)
                eng.tensor_tensor(out=hb[:, s & 1, :, :], in0=z[:, :, :], in1=wide(g1b, l), op=ALU.mult)\
                   .then_inc(hb_chain, 1)
                eng.wait_ge(hb_chain, s + 2)
                eng.tensor_tensor(out=hb[:, s & 1, :, :], in0=hb[:, s & 1, :, :], in1=wide(betab, l), op=ALU.add)\
                   .then_inc(hb_ready, 1)

            def gain2(s, slot, l):
                eng.wait_ge(z2_ready, s + 1)
                eng.tensor_tensor(out=xs[:, slot, :, :], in0=z2[:, :, :], in1=wide(g2b, l), op=ALU.mult)\
                   .then_inc(x_chain, 1)
                eng.wait_ge(x_chain, s + 1)
                eng.tensor_tensor(out=xs[:, slot, :, :], in0=xs[:, slot, :, :], in1=wide(beta2b, l), op=ALU.add)\
                   .then_inc(x_stored, 1)

            def late_low_half(p):
                high, low, _ = halves_of(p)
                eng.wait_ge(late_high, p + 1)
                eng.tensor_tensor(out=low, in0=late[:, p % 2, :], in1=high, op=ALU.subtract).then_inc(late_low, 1)

            def late_mask(n):
                eng.wait_ge(late_edge_ready, 2 * n + 2)
                eng.tensor_tensor(out=mask[:, n + NG_FIRST, :, :], in0=late_edge[:, :, :],
                                  in1=off_diag[:, :].unsqueeze(1).to_broadcast([128, G, N]), op=ALU.mult)\
                   .then_inc(late_mask_done, 1)

            root(var1_ready, rstd1_ready, ve1, rstd1, 0)
            eng.wait_ge(shift_ready, L)
            eng.wait_ge(init_chain, 2)
            gain1(0, 0)

            def step(t, first=False, last=False, masks=False, piece=None):
                if not first:
                    u = t - 1
                    root(var2_ready, rstd2_ready, ve2, rstd2, u)
                    gain2(u, u & (NG - 1), layer(u))
                if masks:
                    late_mask(t - 1)
                if piece is not None:
                    late_low_half(piece)
                if not last:
                    s = t + 1
                    root(var1_ready, rstd1_ready, ve1, rstd1, s)
                    gain1(s, layer(s))

            step(0, first=True)
            for t in range(1, PIECES + 1):
                step(t, masks=True, piece=t - 1)
            with eng.Fori(PIECES + 1, NG - NG_FIRST + 1) as t:
                step(t, masks=True)
            with eng.Fori(NG - NG_FIRST + 1, STEPS - 1) as t:
                step(t)
            step(STEPS - 1, last=True)
            root(var2_ready, rstd2_ready, ve2, rstd2, STEPS - 1)
            gain2(STEPS - 1, NG - 1, L - 1)

        @block.scalar
        def _(eng):
            eng.dma_start(aw[:, :, :], attn_w.partition_broadcast(128)).then_inc(cols_in, 16)
            eng.dma_start(ab[:, :], attn_b.partition_broadcast(128)).then_inc(cols_in, 16)
            for tile, src in ((g1c, g1_down), (beta1c, beta1_down), (b1c, b1_down)):
                eng.dma_start(tile[:, :, :], src).then_inc(cut_in, 16)
            eng.wait_ge(g1c_ready, 1)
            eng.wait_ge(w_in[0], 16)
            for k in range(KD):
                eng.activation(w1h[:, 0, k, :], stage[:, H * k:H * (k + 1)], ACT.Copy,
                               scale=g1c[:, 0, k:k + 1]).then_inc(w_used, 1)
            eng.wait_ge(w_in[1], 16)
            eng.activation(w2h[:, 0, :, :].rearrange("p k h -> p (k h)"), stage[:, KD * H:2 * KD * H],
                           ACT.Copy, scale=WS).then_inc(w_used, 1)

            def late_high_half(p):
                high, _, scale = halves_of(p)
                eng.wait_ge(late_in[p % 2], 16 * (p // 2 + 1))
                if p < KD:
                    eng.wait_ge(shift_ready, 2)
                eng.activation(late[:, p % 2, :], late[:, p % 2, :], ACT.Copy, scale=scale).then_inc(late_scaled, 1)
                eng.wait_ge(late_scaled, p + 1)
                eng.activation(high, late[:, p % 2, :], ACT.Copy).then_inc(late_high, 1)

            def late_edges(n):
                eng.wait_ge(late_adj_in, 16 * (n + 1))
                wait(eng, late_mask_done, n)
                eng.activation(late_edge[:, :, :], late_adj, ACT.Relu).then_inc(late_edge_ready, 1)
                eng.wait_ge(late_edge_ready, 2 * n + 1)
                eng.activation(late_edge[:, :, :], late_edge[:, :, :], ACT.Relu, scale=-1.0, bias=one[:, 0:1])\
                   .then_inc(late_edge_ready, 1)

            def exps(s):
                eng.wait_ge(scores_ready, s + 1)
                for g in range(G):
                    ins = eng.activation(v[:, g, :], v[:, g, :], ACT.Exp, bias=nm[:, g:g + 1],
                                         accum_out=rs[:, g:g + 1])
                ins.then_inc(exp_done, 1)

            def heads(s):
                for k in range(KD):
                    eng.wait_ge(ht_ready, KD * s + k + 1)
                    eng.activation(ht[:, 0, k, :], agg[k][:, :], ACT.Copy).then_inc(hth_done, 1)

            def pt_copy(s):
                eng.wait_ge(pt_ready, s + 1)
                eng.activation(pts[:, :, :].rearrange("p g n -> p (g n)"), sp[:, :], ACT.Copy).then_inc(pt_copied, 1)

            def gelus(t, l, first=False, more=1):
                if not first:
                    eng.wait_ge(ff_ready, G * t)
                for m in range(KH):
                    eng.wait_ge(hid_ready, KH * t + m + 1)
                    if not (first and m < HB):
                        eng.wait_ge(gl_done, KH * t + reuse(m))
                    eng.activation(g32[:, m % HB, :], hid[m % HB][:, :], ACT.Gelu, scale=1.0 / WS,
                                   bias=b1c[:, l, m:m + 1]).then_inc(gelu_done, 1)
                    eng.wait_ge(gelu_done, KH * t + m + 1)
                    eng.activation(gt[:, 0, m, :], g32[:, m % HB, :], ACT.Copy).then_inc(gh_done, 1)
                    if m == PT_AT and more:
                        pt_copy(t + 1)

            exps(0)
            pt_copy(0)
            heads(0)
            exps(1)
            eng.wait_ge(b1_ready, 1)
            gelus(0, 0, first=True)
            heads(1)
            exps(2)
            eng.wait_ge(one_ready, 1)
            late_edges(0)
            late_high_half(0)
            for t in range(1, PIECES):
                gelus(t, layer(t))
                late_edges(t)
                late_high_half(t)
                heads(t + 1)
                exps(t + 2)
            with eng.Fori(PIECES, NG - NG_FIRST) as t:
                gelus(t, layer(t))
                late_edges(t)
                heads(t + 1)
                exps(t + 2)
            with eng.Fori(NG - NG_FIRST, STEPS - 2) as t:
                gelus(t, layer(t))
                heads(t + 1)
                exps(t + 2)
            gelus(STEPS - 2, L - 1)
            heads(STEPS - 1)
            gelus(STEPS - 1, L - 1, more=0)

        @block.tensor
        def _(eng):
            def spread(s):
                eng.wait_ge(cols_done, 2 * G * (s + 1))
                for g in range(G):
                    ins = eng.transpose(sp[:, g * N:(g + 1) * N], sij[:, G + g:G + g + 1].to_broadcast([128, 128]),
                                        ident[:, :])
                ins.then_inc(spread_ready, 1)

            def turn(s):
                eng.wait_ge(exp_done, s + 1)
                for g in range(G):
                    ins = eng.transpose(sp[:, g * N:(g + 1) * N], v[:, g, :], ident[:, :])
                ins.then_inc(pt_ready, 1)

            def gather(s, slot, first=False):
                eng.wait_ge(pt_copied, s + 1)
                eng.wait_ge(x_ready, s + 1)
                if not first:
                    eng.wait_ge(htl_done, KD * s)
                for g in range(G):
                    eng.matmul(pair(agg, g), pts[:, g, :], xs[:, slot, g, :], start=True, stop=True)\
                       .then_inc(agg_ready, 1)

            def shift(l):
                tile = (stage, late[:, :, :].rearrange("p k h -> p (k h)"), last_w1)[l]
                eng.wait_ge(cut_in, 16 * 3)
                for ready in ((w_in[0],), late_in, (last_in,))[l]:
                    eng.wait_ge(ready, 16)
                for m in range(KH):
                    for k in range(KD):
                        ins = eng.matmul(ff[min(l, 1)][:, KH * l + m:KH * l + m + 1], tile[:, H * k + 128 * m:H * k + 128 * (m + 1)],
                                         beta1c[:, l, k:k + 1], start=(k == 0), stop=(k == KD - 1))
                ins.then_inc(shift_ready, 1)

            def heads(s):
                eng.wait_ge(z_ready, s + 1)
                for k in range(KD):
                    for g in range(G):
                        ins = eng.transpose(agg[k][:, g * N:(g + 1) * N], z[:, g, k * 128:(k + 1) * 128], ident[:, :])
                    ins.then_inc(ht_ready, 1)

            def up(t, l, first, more):
                for m in range(KH):
                    if m == 0:
                        eng.wait_ge(htl_done, KD * (t + 1))
                    if not (first and m < HB):
                        eng.wait_ge(gelu_done, KH * t + reuse(m))
                    n = 0
                    for k in range(KD):
                        for w, a in ((w1h, 0), (w1h, 1), (w1l, 0)):
                            ins = eng.matmul(hid[m % HB][:, :], w[:, l, k, m * 128:(m + 1) * 128], ht[:, a, k, :],
                                             start=(n == 0), stop=(n == 3 * KD - 1))
                            n += 1
                    ins.then_inc(hid_ready, 1)
                    if m == PT_AT and more >= 1:
                        turn(t + 1)
                    if m == AGG_AT and more >= 1:
                        gather(t + 1, (t + 1) & (NG - 1))

            def down(t, l, g, first=False):
                if g == 0:
                    eng.wait_ge(b1_ready, L) if first else eng.wait_ge(z2_ready, t)
                for k in range(KH):
                    eng.wait_ge(gh_done, KH * t + k + 1) if g == 0 else None
                    eng.wait_ge(gl_done, KH * t + k + 1) if g == 0 else None
                    for a, w in ((0, w2h), (0, w2l), (1, w2h)):
                        ins = eng.matmul(pair(ff, g), gt[:, a, k, g * N:(g + 1) * N], w[:, l, k, :],
                                         start=(k == 0 and a == 0 and w is w2h), stop=(k == KH - 1 and a == 1))
                ins.then_inc(ff_ready, 1)

            eng.wait_ge(const_ready, 2)
            spread(0)
            shift(0)
            turn(0)
            gather(0, 0, first=True)
            shift(1)
            heads(0)
            shift(2)
            spread(1)

            def step(t, l, first=False, more=2):
                up(t, l, first, more)
                for g in range(G):
                    down(t, l, g, first)
                    if g == 1 and more >= 2:
                        spread(t + 2)
                    if g == G - 2 and more >= 1:
                        heads(t + 1)

            eng.wait_ge(w_used, KD + 1)
            eng.wait_ge(w_split, KD + 1)
            step(0, 0, first=True)
            with eng.Fori(1, STEPS - 2) as t:
                step(t, layer(t))
            step(STEPS - 2, L - 1, more=1)
            step(STEPS - 1, L - 1, more=0)

        @block.vector
        def _(eng):
            def low_halves():
                for k in range(KD):
                    eng.wait_ge(w_used, k + 1)
                    eng.scalar_tensor_tensor(out=w1l[:, 0, k, :], in0=stage[:, H * k:H * (k + 1)],
                                             scalar=g1c[:, 0, k:k + 1], in1=w1h[:, 0, k, :],
                                             op0=ALU.mult, op1=ALU.subtract).then_inc(w_split, 1)
                eng.wait_ge(w_used, KD + 1)
                eng.scalar_tensor_tensor(out=w2l[:, 0, :, :].rearrange("p k h -> p (k h)"),
                                         in0=stage[:, KD * H:2 * KD * H], scalar=WS,
                                         in1=w2h[:, 0, :, :].rearrange("p k h -> p (k h)"),
                                         op0=ALU.mult, op1=ALU.subtract).then_inc(w_split, 1)

            def first_mask(g):
                eng.wait_ge(adj_in[g // 2], 32)
                if g:
                    eng.wait_ge(mask_chain, 2 * g)
                eng.scalar_tensor_tensor(out=edge, in0=adji[g // 2][:, g % 2, :, :], scalar=0.0,
                                         in1=ident[:, :].unsqueeze(1).to_broadcast([128, G, N]),
                                         op0=ALU.is_gt, op1=ALU.max).then_inc(mask_chain, 1)
                eng.wait_ge(mask_chain, 2 * g + 1)
                eng.tensor_scalar(mask[:, g, :, :], edge, 1.0, FAR, ALU.subtract, ALU.mult).then_inc(mask_chain, 1)

            def shift(l):
                eng.wait_ge(shift_ready, L if l else 1)
                eng.tensor_tensor(out=b1c[:, l, :], in0=b1c[:, l, :], in1=ff[min(l, 1)][:, KH * l:KH * (l + 1)], op=ALU.add)\
                   .then_inc(b1_ready, 1)

            eng.wait_ge(const_ready, 2)
            eng.wait_ge(cols_in, 32)

            def cols(s, slot, l, graphs=range(G), first=False):
                eng.wait_ge(x_ready, s + 1)
                for g in graphs:
                    for a in range(2):
                        if not first or g:
                            eng.wait_ge(cols_done, 2 * G * s + 2 * g + a - 1)
                        ins = eng.scalar_tensor_tensor(out=junk[:, a, :], in0=xs[:, slot, g, :], scalar=1.0,
                                                       in1=aw[:, l, a * D:(a + 1) * D], op0=ALU.mult, op1=ALU.mult,
                                                       accum_out=sij[:, a * G + g:a * G + g + 1])
                        ins.then_inc(cols_done, 1)

            def scores(s, l):
                eng.wait_ge(cols_done, 2 * G * (s + 1))
                eng.wait_ge(spread_ready, s + 1)
                eng.scalar_tensor_tensor(out=v[:, :, :], in0=sp[:, :].rearrange("p (g n) -> p g n", g=G),
                                         scalar=ab[:, l:l + 1] if isinstance(l, int) else ab[:, bass.ds(l, 1)],
                                         in1=sij[:, 0:G].unsqueeze(2).to_broadcast([128, G, N]),
                                         op0=ALU.add, op1=ALU.add).then_inc(score_chain, 1)

            def scores_end(s, slot):
                eng.wait_ge(score_chain, 3 * s + 1)
                eng.scalar_tensor_tensor(out=v[:, :, :], in0=v[:, :, :], scalar=SLOPE, in1=v[:, :, :],
                                         op0=ALU.mult, op1=ALU.max).then_inc(score_chain, 1)
                eng.wait_ge(score_chain, 3 * s + 2)
                eng.tensor_tensor(out=v[:, :, :], in0=v[:, :, :], in1=mask[:, slot, :, :], op=ALU.add)\
                   .then_inc(score_chain, 1)
                eng.wait_ge(score_chain, 3 * s + 3)
                eng.tensor_reduce(nm[:, :], v[:, :, :], AX.X, ALU.max, negate=True).then_inc(scores_ready, 1)

            def recip(s):
                eng.wait_ge(exp_done, s + 1)
                eng.reciprocal(rinv[:, :], rs[:, :]).then_inc(rinv_ready, 1)

            def moments(zt, st, mv, ve, chain, base, var_ready):
                for g in range(G):
                    eng.wait_ge(chain, base + G + g)
                    eng.bn_stats(st[:, g, :], zt[:, g, :]).then_inc(chain, 1)
                    if g:
                        ins = eng.bn_aggr(mv[:, g - 1, :], st[:, g - 1, :])
                ins.then_inc(chain, 1)
                eng.wait_ge(chain, base + 2 * G + 1)
                eng.tensor_scalar(ve[:, 0:G - 1], mv[:, 0:G - 1, 1], EPS, None, ALU.add)
                eng.bn_aggr(mv[:, G - 1, :], st[:, G - 1, :]).then_inc(chain, 1)
                eng.wait_ge(chain, base + 2 * G + 2)
                eng.tensor_scalar(ve[:, G - 1:G], mv[:, G - 1:G, 1], EPS, None, ALU.add).then_inc(var_ready, 1)

            def gathered(s, slot, graphs=range(G), first=False):
                if not first and 0 in graphs:
                    eng.wait_ge(hb_ready, s)
                    eng.wait_ge(ht_ready, KD * s)
                eng.wait_ge(rinv_ready, s + 1)
                for g in graphs:
                    eng.wait_ge(agg_ready, G * s + g // 2 * 2 + 2)
                    eng.scalar_tensor_tensor(out=z[:, g, :], in0=pair(agg, g), scalar=rinv[:, g:g + 1],
                                             in1=xs[:, slot, g, :], op0=ALU.mult, op1=ALU.add).then_inc(ln1_chain, 1)

            def norm1(s):
                moments(z, st1, mv1, ve1, ln1_chain, (2 * G + 2) * s, var1_ready)

            def norm1_end(s):
                eng.wait_ge(rstd1_ready, s + 1)
                for g in range(G):
                    ins = eng.tensor_scalar(z[:, g, :], z[:, g, :], mv1[:, g, 0:1], rstd1[:, g:g + 1],
                                            ALU.subtract, ALU.mult)
                ins.then_inc(z_ready, 1)

            def head_low(s):
                for k in range(KD):
                    eng.wait_ge(hth_done, KD * s + k + 1)
                    eng.tensor_tensor(out=ht[:, 1, k, :], in0=agg[k][:, :], in1=ht[:, 0, k, :], op=ALU.subtract)\
                       .then_inc(htl_done, 1)

            def gelu_low(t, m):
                eng.wait_ge(gh_done, KH * t + m + 1)
                eng.tensor_tensor(out=gt[:, 1, m, :], in0=g32[:, m % HB, :], in1=gt[:, 0, m, :], op=ALU.subtract)\
                   .then_inc(gl_done, 1)

            def residual2(t, i, first=False):
                if i == 0:
                    eng.wait_ge(hb_ready, t + 1)
                    if not first:
                        eng.wait_ge(x_stored, t)
                eng.wait_ge(ff_ready, G * t + 2 * i + 2)
                eng.scalar_tensor_tensor(out=z2[:, 2 * i:2 * i + 2, :].rearrange("p g d -> p (g d)"),
                                         in0=ff[i][:, :], scalar=1.0 / WS,
                                         in1=hb[:, t & 1, 2 * i:2 * i + 2, :].rearrange("p g d -> p (g d)"),
                                         op0=ALU.mult, op1=ALU.add).then_inc(ln2_chain, 2)

            def norm2(t):
                moments(z2, st2, mv2, ve2, ln2_chain, (2 * G + 2) * t, var2_ready)

            def norm2_end(t):
                eng.wait_ge(rstd2_ready, t + 1)
                for g in range(G):
                    ins = eng.tensor_scalar(z2[:, g, :], z2[:, g, :], mv2[:, g, 0:1], rstd2[:, g:g + 1],
                                            ALU.subtract, ALU.mult)
                ins.then_inc(z2_ready, 1)

            cols(0, 0, 0, first=True)
            first_mask(0)
            scores(0, 0)
            eng.wait_ge(mask_chain, 2)
            scores_end(0, 0)
            eng.wait_ge(cut_in, 16 * 3)
            eng.tensor_scalar(g1c[:, :, :], g1c[:, :, :], WS, None, ALU.mult).then_inc(g1c_ready, 1)
            for g in range(1, NG_FIRST):
                first_mask(g)
            low_halves()
            eng.wait_ge(mask_chain, 2 * NG_FIRST)
            recip(0)
            gathered(0, 0, first=True)
            norm1(0)
            norm1_end(0)
            head_low(0)
            shift(0)
            cols(1, 1, 0)
            scores(1, 0)
            scores_end(1, 1)
            for l in range(1, L):
                shift(l)

            def step(t, first=False, more=2):
                if not first:
                    residual2(t - 1, 1)
                    norm2(t - 1)
                gelu_low(t, 0)
                gelu_low(t, 1)
                if not first:
                    norm2_end(t - 1)
                for m in range(2, KH):
                    if m == KH - 1 and more >= 1:
                        gathered(t + 1, (t + 1) & (NG - 1), (0,))
                    gelu_low(t, m)
                    if m >= KH - 1 - G and m < KH - 1 and more >= 2:
                        cols(t + 2, (t + 2) & (NG - 1), layer(t + 2), [m - (KH - 1 - G)])
                    if m == KH - 3 and more >= 1:
                        recip(t + 1)
                if more >= 1:
                    gathered(t + 1, (t + 1) & (NG - 1), range(1, G))
                    norm1(t + 1)
                if more >= 2:
                    scores(t + 2, layer(t + 2))
                if more >= 1:
                    norm1_end(t + 1)
                if more >= 2:
                    scores_end(t + 2, (t + 2) & (NG - 1))
                if more >= 1:
                    head_low(t + 1)
                residual2(t, 0, first)

            step(0, first=True)
            with eng.Fori(1, STEPS - 2) as t:
                step(t)
            step(STEPS - 2, more=1)
            step(STEPS - 1, more=0)
            residual2(STEPS - 1, 1)
            norm2(STEPS - 1)
            norm2_end(STEPS - 1)


def wait(eng, sem, value):
    if not isinstance(value, int) or value > 0:
        eng.wait_ge(sem, value)


def other_networks(nc, xs, xin, adji, x_in, adj_in, ident, half, bank, x, adj, w1g, a1g, w2g, bias, w3, b3_down, attn3, out):
    ctx = ExitStack()
    with ctx:
        def sb(name, shape, dt=F32):
            return ctx.enter_context(nc.sbuf_tensor(name, shape, dt))

        sems = {}

        def sem(name):
            sems[name] = ctx.enter_context(nc.semaphore(name))
            return sems[name]

        wf = sb("wf", [128, KD, D])
        wa = sb("wa", [128, KD, 2])
        wm = sb("wm", [128, KD, D])
        biasm = sb("biasm", [128, D], BF16)
        row = sb("row", [128, 8])
        wb = sb("wb", [128, KD, D])
        wat = sb("wat", [128, KD, D])
        bc = sb("bc", [128, KD])
        identb = sb("identb", [128, 128], BF16)
        pick = sb("pick", [128, 4, 32], BF16)
        lab = sb("lab", [128, 4, G, N], BF16)
        r1 = sb("r1", [128, G, D])
        u1 = [sb(f"u1_{i}", [128, G, D]) for i in range(2)]
        u1t = sb("u1t", [128, KD, T])
        wh = sb("wh", [128, G, D])
        ec = sb("ec", [128, 2 * G])
        mkf = sb("mkf", [128, G, N], BF16)
        vf = sb("vf", [128, G, N])
        left = sb("left", [128, G, N])
        top = sb("top", [128, G, 2, 8])
        pause = sb("pause", [128, 1])
        nmf = sb("nmf", [128, G])
        rsf = sb("rsf", [128, G])
        rif = sb("rif", [128, G])
        rif_less = sb("rif_less", [128, G])
        ptf = sb("ptf", [128, G, N])
        negf = sb("negf", [128, G, D])
        posf = sb("posf", [128, G, D])
        r2 = sb("r2", [128, G, D])
        u2 = sb("u2", [128, G, D])
        u2t = sb("u2t", [128, KD, T])
        labt = sb("labt", [128, T], BF16)
        hot = sb("hot", [128, 16, T], BF16)
        cnt = sb("cnt", [128, T], BF16)
        r3 = sb("r3", [128, G, D])
        u3 = [sb(f"u3_{i}", [128, G, D]) for i in range(2)]
        u3t = sb("u3t", [128, KD, T])
        hh = sb("hh", [128, G, D])
        hht = sb("hht", [128, KD, T])
        hat = sb("hat", [128, KD, T])
        mkb = sb("mkb", [128, G, N], BF16)
        vb = sb("vb", [128, G, N])
        nmb = sb("nmb", [128, G])
        rsb = sb("rsb", [128, G])
        rib = sb("rib", [128, G])
        rib_less = sb("rib_less", [128, G])
        ptb = sb("ptb", [128, G, N])
        negb = sb("negb", [128, G, D])
        posb = sb("posb", [128, G, D])
        y = [sb(f"y_{i}", [128, G, D]) for i in range(2)]
        wm2 = y[0][:, :, :].rearrange("p (w k) o -> p w k o", k=KD)
        ab2 = negb[:, 0:2, :]
        bias0, bias1, bias2 = hh[:, 0, :], hh[:, 1, :], hh[:, 2, :]
        part0, part1 = hht[:, 0, 0:128].bitcast(BF16), hht[:, 1, 0:128].bitcast(BF16)

        class Norm:

            def __init__(self, name):
                self.st = sb(name + "_st", [128, G, 6])
                self.mv = sb(name + "_mv", [128, G, 2])
                self.ve = sb(name + "_ve", [128, G])
                self.rstd = sb(name + "_rstd", [128, G])
                self.drop = sb(name + "_drop", [128, G])
                self.shift = sb(name + "_shift", [128, G])
                self.chain = sem(name + "_chain")
                self.var_ready = sem(name + "_var_ready")
                self.rstd_ready = sem(name + "_rstd_ready")
                self.done = sem(name + "_done")
                self.drop_ready = sem(name + "_drop_ready")
                self.shift_ready = sem(name + "_shift_ready")

        n1, n2, n3, n4 = Norm("n1"), Norm("n2"), Norm("n3"), Norm("n4")

        fp, fs = bank[0:2], bank[2]
        mp = bank[3:5]
        bp, bs = bank[5:7], bank[7]

        def pair(banks, g):
            return banks[g // 2][:, (g % 2) * D:(g % 2 + 1) * D]

        def flat(t):
            return t[:, :, :].rearrange("p a b -> p (a b)")

        def half_of(t, i):
            return t[:, 2 * i:2 * i + 2, :].rearrange("p g d -> p (g d)")

        front_in = sem("front_in")
        par_in = sem("par2_in")
        const_ready = sem("const2_ready")
        init_chain = sem("init2_chain")
        pick_chain = sem("pick_chain")
        bias_chain = sem("bias_chain")
        wa_ready = sem("wa_ready")
        r1_ready = sem("r1_ready")
        lab_ready = sem("lab_ready")
        u1_turned, u1t_done = sem("u1_turned"), sem("u1t_done")
        wh_ready, wh_done = sem("wh_ready"), sem("wh_done")
        ec_ready, ec_done = sem("ec_ready"), sem("ec_done")
        fspread = sem("fspread")
        fchain = sem("fchain")
        fscores = sem("fscores")
        fexp = sem("fexp")
        fri = sem("fri")
        ftop_chain = sem("ftop_chain")
        ftop = sem("ftop")
        fturn, fturn_done = sem("fturn"), sem("fturn_done")
        fagg = sem("fagg")
        fneg, fpos, fexpn = sem("fneg"), sem("fpos"), sem("fexpn")
        fsum = sem("fsum")
        u2_raw = sem("u2_raw")
        lab_turned, labt_done = sem("lab_turned"), sem("labt_done")
        hot_ready = sem("hot_ready")
        cnt_ready, cnt_done = sem("cnt_ready"), sem("cnt_done")
        u2_turned, u2t_done = sem("u2_turned"), sem("u2t_done")
        mout = sem("mout")
        r3_ready = sem("r3_ready")
        u3_turned, u3t_done = sem("u3_turned"), sem("u3t_done")
        hht_ready, hht_done = sem("hht_ready"), sem("hht_done")
        hat_ready, hat_done = sem("hat_ready"), sem("hat_done")
        hh_ready, hh_done = sem("hh_ready"), sem("hh_done")
        bsc = sem("bsc")
        bchain = sem("bchain")
        bscores = sem("bscores")
        bexp = sem("bexp")
        bri = sem("bri")
        bturn, bturn_done = sem("bturn"), sem("bturn_done")
        bagg = sem("bagg")
        bneg, bpos, bexpn = sem("bneg"), sem("bpos"), sem("bexpn")
        bsum = sem("bsum")
        y_raw = sem("y_raw")
        out_done = [sem(f"out_done{i}") for i in range(2)]

        block = ctx.enter_context(nc.Block())

        def steps(eng, step, first=-3):
            for i in range(first, 3):
                step(i, i % 2)
            with eng.Fori(0, (NG - 6) // 2) as h:
                step(2 * h + 3, 1)
                step(2 * h + 4, 0)
            for i in range(NG - 3, NG + 1):
                step(i, i % 2)

        def there(s):
            return not isinstance(s, int) or 0 <= s < NG

        @block.sync
        def _(eng):
            def load(s, b):
                eng.dma_start(adji[:, b, :, :], adj[s].rearrange("g i j -> i g j")).then_inc(adj_in[b], 16)
                eng.dma_start(xin[:, b, :, :], x[s].rearrange("g n d -> n g d")).then_inc(x_in[b], 16)

            def store(s, b):
                eng.wait_ge(n4.done, s + 1)
                eng.dma_start(out[s].rearrange("g n d -> n g d"), y[b][:, :, :]).then_inc(out_done[b], 16)

            eng.dma_start(wf[:, :, :], w1g.rearrange("(k p) o -> p k o", p=128)).then_inc(front_in, 16)
            eng.dma_start(ab2[:, :, :], a1g.partition_broadcast(128)).then_inc(front_in, 16)
            for dst, src in (
                (y[0][:, :, :], w2g.rearrange("(w k p) o -> p (w k) o", p=128, k=KD)),
                (wb[:, :, :], w3.rearrange("(k p) o -> p k o", p=128)),
                (wat[:, :, :], attn3.rearrange("(k p) o -> p k o", p=128)),
                (bc[:, :], b3_down),
            ):
                eng.dma_start(dst, src).then_inc(par_in, 16)
            eng.wait_ge(const_ready, 1)
            for c in range(4):
                for a in range(3):
                    eng.dma_start(bias0[32 * c + 4 * a:32 * c + 4 * a + 4, :], bias[c]).then_inc(par_in, 16)

            for s in range(2, 6):
                eng.wait_ge(lab_ready, s - 1)
                eng.wait_ge(r1_ready, s - 1)
                load(s, s % 2)
            with eng.Fori(0, (NG - 6) // 2) as h:
                for b in range(2):
                    eng.wait_ge(lab_ready, 2 * h + 5 + b)
                    eng.wait_ge(r1_ready, 2 * h + 5 + b)
                    load(2 * h + 6 + b, b)
                    store(2 * h + b, b)
            for s in range(NG - 6, NG):
                store(s, s % 2)
            for b in range(2):
                eng.wait_ge(out_done[b], 16 * NG // 2)

        @block.gpsimd
        def _(eng):
            eng.memset(bias0, 0.0).then_inc(const_ready, 1)
            eng.memset(pick[:, :, :], 0.0).then_inc(pick_chain, 1)
            eng.tensor_copy(identb[:, :], ident[:, :]).then_inc(const_ready, 1)
            for a in range(3):
                eng.wait_ge(pick_chain, a + 1)
                eng.affine_select(out=pick[:, :, :], in_=pick[:, :, :], compare_op=ALU.not_equal, fill=1.0,
                                  base=4 * a, pattern=[[1, 4], [-1, 32]], channel_multiplier=0)\
                   .then_inc(pick_chain if a < 2 else const_ready, 1)

            def root(n, s, shift=False):
                if there(s):
                    eng.wait_ge(n.var_ready, s + 1)
                    wait(eng, n.done, s)
                    eng.tensor_tensor(out=n.rstd[:, :], in0=n.ve[:, :], in1=half[:, :], op=ALU.pow)\
                       .then_inc(n.rstd_ready, 1)
                    if shift:
                        eng.tensor_scalar(n.drop[:, :], n.mv[:, :, 0], -1.0, None, ALU.mult)\
                           .then_inc(n.drop_ready, 1)
                        eng.wait_ge(n.rstd_ready, s + 1)
                        eng.wait_ge(n.drop_ready, s + 1)
                        eng.tensor_tensor(out=n.shift[:, :], in0=n.drop[:, :], in1=n.rstd[:, :], op=ALU.mult)\
                           .then_inc(n.shift_ready, 1)

            def enter(s, b):
                if there(s):
                    wait(eng, n1.done, s)
                    eng.wait_ge(x_in[b], 16 * (s // 2 + 1) if isinstance(s, int) else ((s >> 1) + 1) * 16)
                    eng.tensor_tensor(out=r1[:, :, :], in0=xin[:, b, :, :], in1=xs[:, s, :, :], op=ALU.add)\
                       .then_inc(r1_ready, 1)
                    eng.wait_ge(adj_in[b], 16 * (s // 2 + 1) if isinstance(s, int) else ((s >> 1) + 1) * 16)
                    wait(eng, bscores, s - 3)
                    eng.tensor_copy(lab[:, s & 3, :, :], adji[:, b, :, :]).then_inc(lab_ready, 1)

            def add_pos(s, total, total_ready, pos, pos_ready, raw):
                if there(s):
                    eng.wait_ge(total_ready, s + 1)
                    eng.wait_ge(pos_ready, s + 1)
                    eng.tensor_tensor(out=total[:, :, :], in0=total[:, :, :], in1=pos[:, :, :], op=ALU.add)\
                       .then_inc(raw, 1)

            def step(i, own):
                root(n3, i)
                add_pos(i + 1, r2, fsum, posf, fpos, u2_raw)
                enter(i + 3, 1 - own)
                add_pos(i - 1, y[1 - own], bsum, posb, bpos, y_raw)
                root(n2, i + 1)
                root(n1, i + 3, shift=True)
                root(n4, i - 1, shift=True)

            steps(eng, step)

        @block.scalar
        def _(eng):

            def banks_out(s, banks, ready, dst, done, bias_col=None):
                if there(s):
                    for k in range(2):
                        eng.wait_ge(ready, 2 * s + k + 1)
                        if bias_col is None:
                            eng.activation(dst(k), banks[k][:, :], ACT.Copy).then_inc(done, 1)
                        else:
                            eng.activation(dst(k), banks[k][:, :], ACT.Identity, bias=bias_col[:, k:k + 1])\
                               .then_inc(done, 1)

            def one_out(s, src, ready, dst, done):
                if there(s):
                    eng.wait_ge(ready, s + 1)
                    eng.activation(dst, src, ACT.Copy).then_inc(done, 1)

            def exps(s, vt, nm, rs, scores_ready, done):
                if there(s):
                    eng.wait_ge(scores_ready, s + 1)
                    for g in range(G):
                        ins = eng.activation(vt[:, g, :], vt[:, g, :], ACT.Exp, bias=nm[:, g:g + 1],
                                             accum_out=rs[:, g:g + 1])
                    ins.then_inc(done, 1)

            def signs(s, banks, agg_ready, ri, ri_less, ri_ready, pos, pos_ready, pos_read, neg, neg_ready, neg_read):
                if there(s):
                    eng.wait_ge(ri_ready, 2 * s + 2)
                    wait(eng, pos_read, s)
                    wait(eng, neg_read, s)
                    for g in range(G):
                        eng.wait_ge(agg_ready, G * s + g // 2 * 2 + 2)
                        eng.activation(neg[:, g, :], pair(banks, g), ACT.Relu, scale=ri_less[:, g:g + 1])\
                           .then_inc(neg_ready, 1)
                        ins = eng.activation(pos[:, g, :], pair(banks, g), ACT.Relu, scale=ri[:, g:g + 1])
                    ins.then_inc(pos_ready, 1)

            def exp_less(s, neg, neg_ready, expn):
                if there(s):
                    eng.wait_ge(neg_ready, G * s + G)
                    eng.activation(flat(neg), flat(neg), ACT.Exp, scale=-1.0).then_inc(expn, 1)

            def normed(s, n, src, dst, readers):
                if there(s):
                    eng.wait_ge(n.shift_ready, s + 1)
                    for reader, count in readers:
                        wait(eng, reader, count)
                    for g in range(G):
                        ins = eng.activation(dst[:, g, :], src[:, g, :], ACT.Identity, scale=n.rstd[:, g:g + 1],
                                             bias=n.shift[:, g:g + 1])
                    ins.then_inc(n.done, 1)

            def step(i, own):
                one_out(i + 1, mp[0][:, :].bitcast(BF16)[:, 0:T], lab_turned, labt[:, :], labt_done)
                banks_out(i + 2, fp, u1_turned, lambda k: u1t[:, k, :], u1t_done)
                signs(i - 1, bp, bagg, rib, rib_less, bri, posb, bpos, y_raw, negb, bneg, bsum)
                exp_less(i - 1, negb, bneg, bexpn)
                banks_out(i + 2, fp, wh_ready, lambda k: half_of(wh, k), wh_done)
                banks_out(i, bp, u3_turned, lambda k: u3t[:, k, :], u3t_done)
                one_out(i + 2, fs[:, 0:2 * G], ec_ready, ec[:, :], ec_done)
                normed(i - 2, n4, y[own], y[own], [])
                if isinstance(i, int) and i == 0:
                    eng.wait_ge(par_in, 16 * 16)
                banks_out(i, bp, hht_ready, lambda k: hht[:, k, :], hht_done, bc)
                one_out(i + 1, mp[1][:, :], cnt_ready, cnt[:, :], cnt_done)
                exps(i + 2, vf, nmf, rsf, fscores, fexp)
                banks_out(i, bp, hat_ready, lambda k: hat[:, k, :], hat_done)
                banks_out(i + 1, mp, u2_turned, lambda k: u2t[:, k, :], u2t_done)
                one_out(i + 2, fs[:, :], fturn, flat(ptf), fturn_done)
                banks_out(i, bp, hh_ready, lambda k: half_of(hh, k), hh_done)
                exps(i, vb, nmb, rsb, bscores, bexp)
                signs(i + 2, fp, fagg, rif, rif_less, fri, posf, fpos, u2_raw, negf, fneg, fsum)
                one_out(i, bs[:, :], bturn, flat(ptb), bturn_done)
                normed(i + 3, n1, r1, u1[1 - own], [(fsum, i + 2), (u1_turned, 2 * (i + 2))])
                exp_less(i + 2, negf, fneg, fexpn)

            normed(0, n1, r1, u1[0], [])
            steps(eng, step, first=-2)
            normed(NG - 1, n4, y[(NG - 1) % 2], y[(NG - 1) % 2], [])

        @block.tensor
        def _(eng):
            eng.wait_ge(const_ready, 3)
            eng.wait_ge(front_in, 32)
            eng.wait_ge(wa_ready, KD * 2)

            def turn_features(s, src, src_ready, banks, turned, bank_free, free_count):
                if there(s):
                    eng.wait_ge(src_ready, s + 1)
                    wait(eng, bank_free, free_count)
                    for k in range(KD):
                        for g in range(G):
                            ins = eng.transpose(banks[k][:, g * N:(g + 1) * N], src[:, g, k * 128:(k + 1) * 128],
                                                ident[:, :])
                        ins.then_inc(turned, 1)

            def turn_probs(s, src, src_ready, bank_, turned):
                if there(s):
                    eng.wait_ge(src_ready, s + 1)
                    for g in range(G):
                        ins = eng.transpose(bank_[:, g * N:(g + 1) * N], src[:, g, :], ident[:, :])
                    ins.then_inc(turned, 1)

            def turn_labels(s):
                if there(s):
                    eng.wait_ge(lab_ready, s + 1)
                    wait(eng, r3_ready, 2 * s)
                    for g in range(G):
                        ins = eng.transpose(mp[0][:, :].bitcast(BF16)[:, g * N:(g + 1) * N],
                                            lab[:, s & 3, g, :], identb[:, :])
                    ins.then_inc(lab_turned, 1)

            def project(s):
                if there(s):
                    eng.wait_ge(u1t_done, 2 * s + 2)
                    for g in range(G):
                        for k in range(KD):
                            ins = eng.matmul(pair(fp, g), u1t[:, k, g * N:(g + 1) * N], wf[:, k, :],
                                             start=(k == 0), stop=(k == KD - 1))
                        if g % 2:
                            ins.then_inc(wh_ready, 1)

            def score_columns(s):
                if there(s):
                    wait(eng, fturn_done, s)
                    for g in range(G):
                        for k in range(KD):
                            ins = eng.matmul(fs[:, 2 * g:2 * g + 2], u1t[:, k, g * N:(g + 1) * N], wa[:, k, :],
                                             start=(k == 0), stop=(k == KD - 1))
                    ins.then_inc(ec_ready, 1)

            def spread(s):
                if there(s):
                    eng.wait_ge(ec_done, s + 1)
                    for g in range(G):
                        ins = eng.transpose(fs[:, g * N:(g + 1) * N],
                                            ec[:, 2 * g + 1:2 * g + 2].to_broadcast([128, 128]), ident[:, :])
                    ins.then_inc(fspread, 1)

            def gather(s, pt, pt_done, feats, feats_done, feats_count, banks, ready, graphs=range(G)):
                if there(s):
                    eng.wait_ge(pt_done, s + 1)
                    eng.wait_ge(feats_done, feats_count)
                    for g in graphs:
                        eng.matmul(pair(banks, g), pt[:, g, :], feats[:, g, :], start=True, stop=True)\
                           .then_inc(ready, 1)

            def count(s):
                if there(s):
                    for q in range(4):
                        eng.wait_ge(hot_ready, 4 * s + q + 1)
                        for c in range(4):
                            ins = eng.matmul(mp[1][32 * c:32 * c + 32, :], pick[:, q, :], hot[:, 4 * q + c, :],
                                             start=(q == 0), stop=(q == 3), tile_position=(0, 32 * c))
                    ins.then_inc(cnt_ready, 1)

            def mid(s, a):
                if there(s):
                    eng.wait_ge(u2t_done, 2 * s + 2)
                    eng.wait_ge(cnt_done, s + 1)
                    for g in (2 * a, 2 * a + 1):
                        for k in range(KD):
                            eng.matmul(pair(mp, g), u2t[:, k, g * N:(g + 1) * N], wm[:, k, :],
                                       start=(k == 0), stop=False)
                        ins = eng.matmul(pair(mp, g), cnt[:, g * N:(g + 1) * N], biasm[:, :], start=False, stop=True)
                        if g % 2:
                            ins.then_inc(mout, 1)

            def across(s, o, w, src, src_done, done):
                if there(s):
                    eng.wait_ge(src_done, 2 * s + 2)
                    for k in range(KD):
                        ins = eng.matmul(bp[o][:, :], w[:, k, o * 128:(o + 1) * 128], src[:, k, :],
                                         start=(k == 0), stop=(k == KD - 1))
                    ins.then_inc(done, 1)

            def turn_back(s):
                if there(s):
                    eng.wait_ge(hat_done, 2 * s + 2)
                    for g in range(G):
                        for k in range(KD):
                            ins = eng.transpose(pair(bp, g)[:, k * 128:(k + 1) * 128], hht[:, k, g * N:(g + 1) * N],
                                                ident[:, :])
                        if g % 2:
                            ins.then_inc(hh_ready, 1)

            def back_scores(s):
                if there(s):
                    wait(eng, bturn_done, s)
                    eng.wait_ge(hat_done, 2 * s + 2)
                    for g in range(G):
                        for k in range(KD):
                            ins = eng.matmul(bs[:, g * N:(g + 1) * N], hat[:, k, g * N:(g + 1) * N],
                                             hht[:, k, g * N:(g + 1) * N], start=(k == 0), stop=(k == KD - 1))
                    ins.then_inc(bsc, 1)

            def step(i, own):
                f, m, b = i + 2, i + 1, i
                if isinstance(i, int) and i == -1:
                    eng.wait_ge(wa_ready, KD * 2 + 2)
                    eng.wait_ge(par_in, 16 * 16)
                gather(b - 1, ptb, bturn_done, hh, hh_done, 2 * b, bp, bagg, (0, 1))
                turn_labels(m)
                turn_features(f, u1[own], n1.done, fp, u1_turned, fpos, f)
                gather(b - 1, ptb, bturn_done, hh, hh_done, 2 * b, bp, bagg, (2, 3))
                project(f)
                turn_features(b, u3[own], n3.done, bp, u3_turned, bpos, b)
                score_columns(f)
                across(b, 0, wb, u3t, u3t_done, hht_ready)
                spread(f)
                across(b, 1, wb, u3t, u3t_done, hht_ready)
                count(m)
                across(b, 0, wat, hht, hht_done, hat_ready)
                across(b, 1, wat, hht, hht_done, hat_ready)
                if there(m):
                    eng.wait_ge(labt_done, m + 1)
                    eng.wait_ge(cnt_done, m + 1)
                turn_features(m, u2, n2.done, mp, u2_turned, r3_ready, 2 * m)
                back_scores(b)
                turn_probs(f, vf, ftop, fs, fturn)
                turn_back(b)
                gather(f, ptf, fturn_done, wh, wh_done, 2 * f + 2, fp, fagg)
                mid(m, 0)
                turn_probs(b, vb, bexp, bs, bturn)
                mid(m, 1)

            steps(eng, step)

        @block.vector
        def _(eng):
            def moments(s, n, src, ready):
                if there(s):
                    eng.wait_ge(ready, s + 1)
                    base = (G + 2) * s
                    for g in range(G):
                        if g:
                            eng.wait_ge(n.chain, base + g)
                        eng.bn_stats(n.st[:, g, :], src[:, g, :]).then_inc(n.chain, 1)
                        if g:
                            ins = eng.bn_aggr(n.mv[:, g - 1, :], n.st[:, g - 1, :])
                    ins.then_inc(n.chain, 1)
                    eng.wait_ge(n.chain, base + G + 1)
                    eng.tensor_scalar(n.ve[:, 0:G - 1], n.mv[:, 0:G - 1, 1], EPS, None, ALU.add)
                    eng.bn_aggr(n.mv[:, G - 1, :], n.st[:, G - 1, :]).then_inc(n.chain, 1)
                    eng.wait_ge(n.chain, base + G + 2)
                    eng.tensor_scalar(n.ve[:, G - 1:G], n.mv[:, G - 1:G, 1], EPS, None, ALU.add)\
                       .then_inc(n.var_ready, 1)

            def normed(s, n, src, dst, readers=()):
                if there(s):
                    eng.wait_ge(n.rstd_ready, s + 1)
                    for reader, count in readers:
                        wait(eng, reader, count)
                    for g in range(G):
                        ins = eng.tensor_scalar(dst[:, g, :], src[:, g, :], n.mv[:, g, 0:1], n.rstd[:, g:g + 1],
                                                ALU.subtract, ALU.mult)
                    ins.then_inc(n.done, 1)

            def hots(s, part):
                if there(s):
                    eng.wait_ge(labt_done, s + 1)
                    wait(eng, cnt_ready, s)
                    for l in range(4 * part, 4 * part + 4):
                        ins = eng.tensor_scalar(hot[:, l, :], labt[:, :], float(l), None, ALU.is_equal)
                    ins.then_inc(hot_ready, 1)

            def front_scores(s):
                if there(s):
                    eng.wait_ge(lab_ready, s + 1)
                    eng.tensor_scalar(mkf[:, :, :], lab[:, s & 3, :, :], 0.0, -3e38, ALU.is_equal, ALU.mult)\
                       .then_inc(fchain, 1)
                    eng.wait_ge(fspread, s + 1)
                    wait(eng, fturn, s)
                    src = ec[:, :].rearrange("p (g c) -> p g c", c=2)[:, :, 0:1].to_broadcast([128, G, N])
                    eng.tensor_tensor(out=vf[:, :, :], in0=fs[:, :].rearrange("p (g n) -> p g n", g=G),
                                      in1=src, op=ALU.add).then_inc(fchain, 1)
                    eng.wait_ge(fchain, 4 * s + 2)
                    eng.scalar_tensor_tensor(out=vf[:, :, :], in0=vf[:, :, :], scalar=SLOPE, in1=vf[:, :, :],
                                             op0=ALU.mult, op1=ALU.max).then_inc(fchain, 1)
                    eng.wait_ge(fchain, 4 * s + 3)
                    eng.scalar_tensor_tensor(out=vf[:, :, :], in0=mkf[:, :, :], scalar=FAR / 3e38, in1=vf[:, :, :],
                                             op0=ALU.mult, op1=ALU.add).then_inc(fchain, 1)
                    eng.wait_ge(fchain, 4 * s + 4)
                    eng.tensor_reduce(nmf[:, :], vf[:, :, :], AX.X, ALU.max, negate=True).then_inc(fscores, 1)

            def largest(s):
                if there(s):
                    eng.wait_ge(fexp, s + 1)
                    eng.reciprocal(rif[:, :], rsf[:, :]).then_inc(fri, 1)
                    for g in range(G):
                        ins = eng.max(top[:, g, 0, :], vf[:, g, :])
                    ins.then_inc(ftop_chain, 1)
                    eng.wait_ge(fri, 2 * s + 1)
                    eng.tensor_scalar(rif_less[:, :], rif[:, :], -1.0, None, ALU.mult).then_inc(fri, 1)
                    eng.wait_ge(ftop_chain, 5 * s + 1)
                    eng.memset(pause[:, 0:1], 0.0).then_inc(ftop_chain, 1)
                    for g in range(G):
                        ins = eng.match_replace(left[:, g, :], top[:, g, 0, :], vf[:, g, :], -1.0)
                    ins.then_inc(ftop_chain, 1)
                    eng.wait_ge(ftop_chain, 5 * s + 3)
                    eng.memset(pause[:, 0:1], 0.0).then_inc(ftop_chain, 1)
                    for g in range(G):
                        ins = eng.max(top[:, g, 1, :], left[:, g, :])
                    ins.then_inc(ftop_chain, 1)
                    eng.wait_ge(ftop_chain, 5 * s + 5)
                    for g in range(G):
                        ins = eng.scalar_tensor_tensor(out=vf[:, g, :], in0=vf[:, g, :], scalar=top[:, g, 1, 7:8],
                                                       in1=vf[:, g, :], op0=ALU.is_ge, op1=ALU.mult)
                    ins.then_inc(ftop, 1)

            def less_one(s, neg, expn, base, dst, sum_ready, readers=()):
                if there(s):
                    eng.wait_ge(expn, s + 1)
                    for reader, count in readers:
                        wait(eng, reader, count)
                    eng.scalar_tensor_tensor(out=flat(dst), in0=flat(neg), scalar=-1.0, in1=flat(base),
                                             op0=ALU.add, op1=ALU.add).then_inc(sum_ready, 1)

            def mid_sum(s):
                if there(s):
                    for k in range(2):
                        eng.wait_ge(mout, 2 * s + k + 1)
                        eng.scalar_tensor_tensor(out=half_of(r3, k), in0=half_of(u2, k), scalar=2.0,
                                                 in1=mp[k][:, :], op0=ALU.mult, op1=ALU.add).then_inc(r3_ready, 1)

            def back_softmax(s):
                if there(s):
                    eng.tensor_scalar(mkb[:, :, :], lab[:, s & 3, :, :], 0.0, -3e38, ALU.is_equal, ALU.mult)\
                       .then_inc(bchain, 1)
                    eng.wait_ge(bchain, 2 * s + 1)
                    wait(eng, bturn, s)
                    eng.wait_ge(bsc, s + 1)
                    eng.tensor_tensor(out=vb[:, :, :], in0=mkb[:, :, :],
                                      in1=bs[:, :].rearrange("p (g n) -> p g n", g=G), op=ALU.add).then_inc(bchain, 1)
                    eng.wait_ge(bchain, 2 * s + 2)
                    eng.tensor_reduce(nmb[:, :], vb[:, :, :], AX.X, ALU.max, negate=True).then_inc(bscores, 1)

            def back_recip(s):
                if there(s):
                    eng.wait_ge(bexp, s + 1)
                    eng.reciprocal(rib[:, :], rsb[:, :]).then_inc(bri, 1)
                    eng.wait_ge(bri, 2 * s + 1)
                    eng.tensor_scalar(rib_less[:, :], rib[:, :], -1.0, None, ALU.mult).then_inc(bri, 1)

            def step(i, own):
                f, m, b = i + 2, i + 1, i
                if there(b):
                    eng.wait_ge(r3_ready, 2 * b + 2)
                moments(b, n3, r3, n2.done)
                less_one(f - 1, negf, fexpn, u1[1 - own], r2, fsum, [(n2.done, f - 1)])
                hots(m, 0)
                normed(b, n3, r3, u3[own], [(bsum, b - 1), (u3_turned, 2 * b - 2)])
                hots(m, 1)
                hots(m, 2)
                less_one(b - 1, negb, bexpn, u3[1 - own], y[1 - own], bsum,
                         [(out_done[1 - own], ((b - 1) >> 1) * 16)])
                hots(m, 3)
                moments(m, n2, r2, u2_raw)
                front_scores(f)
                normed(m, n2, r2, u2, [(r3_ready, 2 * m), (u2_turned, 2 * m)])
                largest(f)
                back_softmax(b)
                moments(f + 1, n1, r1, r1_ready)
                back_recip(b)
                moments(b - 1, n4, y[1 - own], y_raw)
                mid_sum(m)

            moments(0, n1, r1, r1_ready)
            eng.wait_ge(front_in, 32)
            for k in range(KD):
                for a in range(2):
                    eng.scalar_tensor_tensor(out=negf[:, 2 * k + a, :], in0=wf[:, k, :], scalar=1.0,
                                             in1=ab2[:, a, :], op0=ALU.mult, op1=ALU.mult,
                                             accum_out=wa[:, k, a:a + 1]).then_inc(wa_ready, 1)
            eng.wait_ge(par_in, 16 * 16)
            eng.tensor_tensor(out=flat(wm), in0=wm2[:, 0, :, :].rearrange("p k o -> p (k o)"),
                              in1=wm2[:, 1, :, :].rearrange("p k o -> p (k o)"), op=ALU.add).then_inc(wa_ready, 1)
            eng.tensor_reduce(row[:, :], ident[:, :].rearrange("p (c a q) -> p a c q", c=4, q=4), AX.XY, ALU.add)\
               .then_inc(bias_chain, 1)
            eng.tensor_scalar(part0, bias0, 1.0, None, ALU.mult).then_inc(bias_chain, 1)
            eng.wait_ge(bias_chain, 2)
            eng.tensor_tensor(out=bias1, in0=bias0, in1=part0, op=ALU.subtract).then_inc(bias_chain, 1)
            eng.wait_ge(bias_chain, 3)
            eng.tensor_scalar(part1, bias1, 1.0, None, ALU.mult).then_inc(bias_chain, 1)
            eng.tensor_scalar(biasm[:, :], part0, row[:, 0:1], None, ALU.mult).then_inc(bias_chain, 1)
            eng.wait_ge(bias_chain, 5)
            eng.tensor_tensor(out=bias2, in0=bias1, in1=part1, op=ALU.subtract).then_inc(bias_chain, 1)
            eng.scalar_tensor_tensor(out=biasm[:, :], in0=part1, scalar=row[:, 1:2], in1=biasm[:, :],
                                     op0=ALU.mult, op1=ALU.add).then_inc(bias_chain, 1)
            eng.wait_ge(bias_chain, 7)
            eng.scalar_tensor_tensor(out=biasm[:, :], in0=bias2, scalar=row[:, 2:3], in1=biasm[:, :],
                                     op0=ALU.mult, op1=ALU.add).then_inc(wa_ready, 1)
            eng.wait_ge(wa_ready, 6)

            steps(eng, step, first=-2)


def layer(s):
    return s // NG if isinstance(s, int) else (s >> (NG.bit_length() - 1)).with_bounds(min_val=0, max_val=L - 1)


def reuse(m):
    held = [i for i in range(KH) if i % HB == m % HB]
    return m - HB + 1 if m >= HB else held[-1] - KH + 1


def build(nc, x, adj, first, others, out):
    with (
        nc.sbuf_tensor("xs", [128, NG, G, D], F32) as xs,
        nc.sbuf_tensor("xin", [128, 2, G, D], F32) as xin,
        nc.sbuf_tensor("adji", [128, 2, G, N], I32) as adji,
        nc.sbuf_tensor("ident", [128, 128], F32) as ident,
        nc.sbuf_tensor("half", [128, G], F32) as half,
        ExitStack() as ctx,
    ):
        bank = [ctx.enter_context(nc.psum_tensor(f"bank{i}", [128, T], F32)) for i in range(8)]
        x_in = [ctx.enter_context(nc.semaphore(f"x2_in{i}")) for i in range(2)]
        adj_in = [ctx.enter_context(nc.semaphore(f"adj2_in{i}")) for i in range(2)]
        first_network(nc, xs, xin, adji, x_in, adj_in, ident, half, bank, x, adj, *first)
        other_networks(nc, xs, xin, adji, x_in, adj_in, ident, half, bank, x, adj, *others, out)


def kernel(**inputs):
    import numpy as np
    import concourse.bacc as bacc
    from concourse.bass_utils import run_bass_kernel_spmd as run

    nc = bacc.Bacc("TRN2", target_bir_lowering=False, num_devices=1)
    arrays = {}

    def give(name, shape=None, order=None, as_name=None):
        a = np.asarray(inputs[name])
        if shape:
            a = a.reshape(shape)
        if order:
            a = a.transpose(order)
        name = "in_" + (as_name or name)
        arrays[name] = np.ascontiguousarray(a)
        return nc.dram_tensor(name, a.shape, mybir.dt.from_np(a.dtype), kind="ExternalInput").ap()

    def down(name):
        return give(name, (L, -1, 128), (2, 0, 1), name + "_down")

    x = give("x", (NG, G, N, D))
    adj = give("adj", (NG, G, N, N))
    first = [give("L0_gnn_attn_w"), give("L0_gnn_attn_b"), give("L0_gnn_W1"), down("L0_gnn_b1"), give("L0_gnn_W2"),
             give("L0_gnn_b2"), give("L0_gnn_g1"), give("L0_gnn_beta1"), give("L0_gnn_g2"), give("L0_gnn_beta2"),
             down("L0_gnn_g1"), down("L0_gnn_beta1")]
    others = [give("L1_gnn_W"), give("L1_gnn_a", (2, D)),
              give("L2_gnn_weights", (2, D, D), (0, 2, 1)).rearrange("w i o -> (w i) o"),
              give("L2_gnn_bias", (4, 4, D), (1, 0, 2)),
              give("L3_gnn_W", None, (1, 0)), give("L3_gnn_b", (KD, 128), (1, 0), "b3_down"),
              give("L3_gnn_attn")]
    out = nc.dram_tensor("out", (NG, G, N, D), F32, kind="ExternalOutput").ap()
    build(nc, x, adj, first, others, out)
    r = run(nc, [arrays], core_ids=[0])
    return r.results[0]["out"].reshape(B, N, D)
```
